# Optimizing a Trainium2 kernel written in Bass

```python
import numpy as np
import jax
import jax.numpy as jnp

def _softmax(x, axis=-1):
    return jax.nn.softmax(x, axis=axis)

def _gelu(x):
    return jax.nn.gelu(x, approximate=True)

def _silu(x):
    return jax.nn.silu(x)

def _sigmoid(x):
    return jax.nn.sigmoid(x)

def _layernorm(x, axis=-1, eps=1e-05):
    m = jnp.mean(x, axis=axis, keepdims=True)
    v = jnp.var(x, axis=axis, keepdims=True)
    return (x - m) / jnp.sqrt(v + eps)

def _scatter_add(tgt, idx, src, axis=0):
    return tgt.at[idx].add(src)

def _segment_sum(src, seg, n):
    return jax.ops.segment_sum(src, seg, n)
kernel_name = 'mk_vit_tower_d2_tok_img256_r4_0e9126'

def setup_inputs(seed: int=0):
    np.random.seed(seed)
    _w = jnp.asarray

    def _rec_inputs():
        import jax
        import jax.numpy as jnp
        _rk = jax.random.key(seed)
        x = -0.000596345 + 1.00056 * jax.random.normal(jax.random.fold_in(_rk, 1), (64, 64, 64, 3), jnp.float32)
        return x
    x = _rec_inputs()

    def _L0_tok_setup():
        import jax, jax.numpy as jnp
        import numpy as np
        B, H, W = (16, 64, 64)
        WIDTH, LAYERS, M1, M2 = (32, 4, 12, 12)
        EPS = 1e-05

        def layer_norm(x, g, b):
            mu = jnp.mean(x, axis=-1, keepdims=True)
            var = jnp.mean((x - mu) ** 2, axis=-1, keepdims=True)
            return (x - mu) * jax.lax.rsqrt(var + EPS) * g + b

        def gelu(x):
            return jax.nn.gelu(x, approximate=False)

        def spectral_conv(x, w1, w2):
            b, c, h, w = x.shape
            x_ft = jnp.fft.rfft2(x)
            out_ft = jnp.zeros((b, w1.shape[1], h, w // 2 + 1), dtype=x_ft.dtype)
            out_ft = out_ft.at[:, :, :M1, :M2].set(jnp.einsum('bixy,ioxy->boxy', x_ft[:, :, :M1, :M2], w1))
            out_ft = out_ft.at[:, :, -M1:, :M2].set(jnp.einsum('bixy,ioxy->boxy', x_ft[:, :, -M1:, :M2], w2))
            return jnp.fft.irfft2(out_ft, s=(h, w))
        key = jax.random.key(seed)
        ks = jax.random.split(key, 16)
        scale = 1.0 / (WIDTH * WIDTH)
        d = {'x': jax.random.normal(ks[0], (B, H, W, 3), jnp.float32), 'fc0_w': jax.random.normal(ks[1], (3, WIDTH), jnp.float32) * 0.5, 'fc0_b': jnp.zeros((WIDTH,), jnp.float32), 'ln0_g': jnp.ones((WIDTH,), jnp.float32), 'ln0_b': jnp.zeros((WIDTH,), jnp.float32), 'w1r': jax.random.uniform(ks[2], (LAYERS, WIDTH, WIDTH, M1, M2), jnp.float32) * scale, 'w1i': jax.random.uniform(ks[3], (LAYERS, WIDTH, WIDTH, M1, M2), jnp.float32) * scale, 'w2r': jax.random.uniform(ks[4], (LAYERS, WIDTH, WIDTH, M1, M2), jnp.float32) * scale, 'w2i': jax.random.uniform(ks[5], (LAYERS, WIDTH, WIDTH, M1, M2), jnp.float32) * scale, 'conv_w': jax.random.normal(ks[6], (LAYERS, WIDTH, WIDTH), jnp.float32) * (1.0 / np.sqrt(WIDTH)), 'conv_b': jnp.zeros((LAYERS, WIDTH), jnp.float32), 'ln_g': jnp.ones((LAYERS, WIDTH), jnp.float32), 'ln_b': jnp.zeros((LAYERS, WIDTH), jnp.float32), 'fc1_w': jax.random.normal(ks[7], (WIDTH, 128), jnp.float32) * (1.0 / np.sqrt(WIDTH)), 'fc1_b': jnp.zeros((128,), jnp.float32), 'fc2_w': jax.random.normal(ks[8], (128, 64), jnp.float32) * (1.0 / np.sqrt(128)), 'fc2_b': jnp.zeros((64,), jnp.float32), 'fc3_w': jax.random.normal(ks[9], (64, 1), jnp.float32) * (1.0 / np.sqrt(64)), 'fc3_b': jnp.zeros((1,), jnp.float32)}
        return d
    _L0_tok_all = _L0_tok_setup()
    _L0_tok_in = {k: v for k, v in _L0_tok_all.items() if k in ('fc0_w', 'fc0_b', 'ln0_g', 'ln0_b', 'w1r', 'w1i', 'w2r', 'w2i', 'conv_w', 'conv_b', 'ln_g', 'ln_b', 'fc1_w', 'fc1_b', 'fc2_w', 'fc2_b', 'fc3_w', 'fc3_b')}
    del _L0_tok_all

    def _L0_attn_setup():
        import jax, jax.numpy as jnp
        import numpy as np
        B, N, D, H = (4, 256, 64, 8)
        key = jax.random.key(seed)
        k1, k2, k3 = jax.random.split(key, 3)
        x = jax.random.normal(k1, (B, N, D), dtype=jnp.float32)
        Wqkv = jax.random.normal(k2, (D, 3 * D * H), dtype=jnp.float32) * 0.02
        bqkv = jnp.zeros((3 * D * H,), dtype=jnp.float32)
        W0 = jax.random.normal(k3, (D * H, D), dtype=jnp.float32) * 0.02
        b0 = jnp.zeros((D,), dtype=jnp.float32)
        return {'x': x, 'Wqkv': Wqkv, 'bqkv': bqkv, 'W0': W0, 'b0': b0}
    _L0_attn_all = _L0_attn_setup()
    _L0_attn_in = {k: v for k, v in _L0_attn_all.items() if k in ('Wqkv', 'bqkv', 'W0', 'b0')}
    del _L0_attn_all

    def _L0_ffn_setup():
        import jax, jax.numpy as jnp
        import numpy as np
        C = 64
        HID = 256
        E = 8
        TEMP = 1.0
        key = jax.random.key(seed)
        ks = jax.random.split(key, 7)
        x = jax.random.normal(ks[0], (8, 4096, C), dtype=jnp.float32)
        W1 = jax.random.normal(ks[1], (C, HID), dtype=jnp.float32) * 0.02
        b1 = jnp.zeros((HID,), dtype=jnp.float32)
        Wg = jax.random.normal(ks[2], (HID, E), dtype=jnp.float32) * 0.02
        bg = jnp.zeros((E,), dtype=jnp.float32)
        Wd = jax.random.normal(ks[3], (E, HID, C), dtype=jnp.float32) * 0.02
        bd = jnp.zeros((E, C), dtype=jnp.float32)
        return {'x': x, 'W1': W1, 'b1': b1, 'Wg': Wg, 'bg': bg, 'Wd': Wd, 'bd': bd}
    _L0_ffn_all = _L0_ffn_setup()
    _L0_ffn_in = {k: v for k, v in _L0_ffn_all.items() if k in ('W1', 'b1', 'Wg', 'bg', 'Wd', 'bd')}
    del _L0_ffn_all

    def _L1_attn_setup():
        import jax, jax.numpy as jnp
        import numpy as np
        U_DECAY = 0.97
        X_DECAY = 0.97
        LN_EPS = 1e-05
        L1_EPS = 1e-12

        def _ln(x):
            m = jnp.mean(x, axis=-1, keepdims=True)
            v = jnp.mean((x - m) ** 2, axis=-1, keepdims=True)
            return (x - m) * jax.lax.rsqrt(v + LN_EPS)
        key = jax.random.key(seed)
        k0, k1, k2, k3 = jax.random.split(key, 4)
        B, T, d, n = (8, 64, 64, 256)
        embeddings = jax.random.normal(k0, (B, T, d), dtype=jnp.float32)
        E = jax.random.normal(k1, (d, n), dtype=jnp.float32) / n ** 0.5
        Dx = jax.random.normal(k2, (n, d), dtype=jnp.float32) / d ** 0.5
        Dy = jax.random.normal(k3, (n, d), dtype=jnp.float32) / d ** 0.5
        return {'embeddings': embeddings, 'E': E, 'Dx': Dx, 'Dy': Dy}
    _L1_attn_all = _L1_attn_setup()
    _L1_attn_in = {k: v for k, v in _L1_attn_all.items() if k in ('E', 'Dx', 'Dy')}
    del _L1_attn_all

    def _L1_ffn_setup():
        import jax, jax.numpy as jnp
        import numpy as np
        D_MODEL = 64
        EXPERT_DIM = 128
        NUM_EXPERTS = 8
        TOP_K = 2
        SEQ_LEN = 512
        BATCH = 2
        key = jax.random.key(seed)
        ks = jax.random.split(key, 8)
        s = 0.02
        x = jax.random.normal(ks[0], (SEQ_LEN, BATCH, D_MODEL), dtype=jnp.float32)
        Wg = jax.random.normal(ks[1], (D_MODEL, NUM_EXPERTS), dtype=jnp.float32) * s
        bg = jax.random.normal(ks[2], (NUM_EXPERTS,), dtype=jnp.float32) * s
        bias = jnp.zeros((NUM_EXPERTS,), dtype=jnp.float32)
        W1 = jax.random.normal(ks[3], (NUM_EXPERTS, D_MODEL, EXPERT_DIM), dtype=jnp.float32) * s
        b1 = jax.random.normal(ks[4], (NUM_EXPERTS, EXPERT_DIM), dtype=jnp.float32) * s
        W2 = jax.random.normal(ks[5], (NUM_EXPERTS, EXPERT_DIM, D_MODEL), dtype=jnp.float32) * s
        b2 = jax.random.normal(ks[6], (NUM_EXPERTS, D_MODEL), dtype=jnp.float32) * s
        return {'x': x, 'Wg': Wg, 'bg': bg, 'bias': bias, 'W1': W1, 'b1': b1, 'W2': W2, 'b2': b2}
    _L1_ffn_all = _L1_ffn_setup()
    _L1_ffn_in = {k: v for k, v in _L1_ffn_all.items() if k in ('Wg', 'bg', 'bias', 'W1', 'b1', 'W2', 'b2')}
    del _L1_ffn_all
    return {'x': x, 'L0_tok_fc0_w': _L0_tok_in['fc0_w'], 'L0_tok_fc0_b': _L0_tok_in['fc0_b'], 'L0_tok_ln0_g': _L0_tok_in['ln0_g'], 'L0_tok_ln0_b': _L0_tok_in['ln0_b'], 'L0_tok_w1r': _L0_tok_in['w1r'], 'L0_tok_w1i': _L0_tok_in['w1i'], 'L0_tok_w2r': _L0_tok_in['w2r'], 'L0_tok_w2i': _L0_tok_in['w2i'], 'L0_tok_conv_w': _L0_tok_in['conv_w'], 'L0_tok_conv_b': _L0_tok_in['conv_b'], 'L0_tok_ln_g': _L0_tok_in['ln_g'], 'L0_tok_ln_b': _L0_tok_in['ln_b'], 'L0_tok_fc1_w': _L0_tok_in['fc1_w'], 'L0_tok_fc1_b': _L0_tok_in['fc1_b'], 'L0_tok_fc2_w': _L0_tok_in['fc2_w'], 'L0_tok_fc2_b': _L0_tok_in['fc2_b'], 'L0_tok_fc3_w': _L0_tok_in['fc3_w'], 'L0_tok_fc3_b': _L0_tok_in['fc3_b'], 'L0_attn_Wqkv': _L0_attn_in['Wqkv'], 'L0_attn_bqkv': _L0_attn_in['bqkv'], 'L0_attn_W0': _L0_attn_in['W0'], 'L0_attn_b0': _L0_attn_in['b0'], 'L0_ffn_W1': _L0_ffn_in['W1'], 'L0_ffn_b1': _L0_ffn_in['b1'], 'L0_ffn_Wg': _L0_ffn_in['Wg'], 'L0_ffn_bg': _L0_ffn_in['bg'], 'L0_ffn_Wd': _L0_ffn_in['Wd'], 'L0_ffn_bd': _L0_ffn_in['bd'], 'L1_attn_E': _L1_attn_in['E'], 'L1_attn_Dx': _L1_attn_in['Dx'], 'L1_attn_Dy': _L1_attn_in['Dy'], 'L1_ffn_Wg': _L1_ffn_in['Wg'], 'L1_ffn_bg': _L1_ffn_in['bg'], 'L1_ffn_bias': _L1_ffn_in['bias'], 'L1_ffn_W1': _L1_ffn_in['W1'], 'L1_ffn_b1': _L1_ffn_in['b1'], 'L1_ffn_W2': _L1_ffn_in['W2'], 'L1_ffn_b2': _L1_ffn_in['b2']}

def reference(x, L0_tok_fc0_w, L0_tok_fc0_b, L0_tok_ln0_g, L0_tok_ln0_b, L0_tok_w1r, L0_tok_w1i, L0_tok_w2r, L0_tok_w2i, L0_tok_conv_w, L0_tok_conv_b, L0_tok_ln_g, L0_tok_ln_b, L0_tok_fc1_w, L0_tok_fc1_b, L0_tok_fc2_w, L0_tok_fc2_b, L0_tok_fc3_w, L0_tok_fc3_b, L0_attn_Wqkv, L0_attn_bqkv, L0_attn_W0, L0_attn_b0, L0_ffn_W1, L0_ffn_b1, L0_ffn_Wg, L0_ffn_bg, L0_ffn_Wd, L0_ffn_bd, L1_attn_E, L1_attn_Dx, L1_attn_Dy, L1_ffn_Wg, L1_ffn_bg, L1_ffn_bias, L1_ffn_W1, L1_ffn_b1, L1_ffn_W2, L1_ffn_b2):
    import jax
    import jax.numpy as jnp

    def _L0_tok_ref(x, fc0_w, fc0_b, ln0_g, ln0_b, w1r, w1i, w2r, w2i, conv_w, conv_b, ln_g, ln_b, fc1_w, fc1_b, fc2_w, fc2_b, fc3_w, fc3_b):
        import jax, jax.numpy as jnp
        import numpy as np
        B, H, W = (16, 64, 64)
        WIDTH, LAYERS, M1, M2 = (32, 4, 12, 12)
        EPS = 1e-05

        def layer_norm(x, g, b):
            mu = jnp.mean(x, axis=-1, keepdims=True)
            var = jnp.mean((x - mu) ** 2, axis=-1, keepdims=True)
            return (x - mu) * jax.lax.rsqrt(var + EPS) * g + b

        def gelu(x):
            return jax.nn.gelu(x, approximate=False)

        def spectral_conv(x, w1, w2):
            b, c, h, w = x.shape
            x_ft = jnp.fft.rfft2(x)
            out_ft = jnp.zeros((b, w1.shape[1], h, w // 2 + 1), dtype=x_ft.dtype)
            out_ft = out_ft.at[:, :, :M1, :M2].set(jnp.einsum('bixy,ioxy->boxy', x_ft[:, :, :M1, :M2], w1))
            out_ft = out_ft.at[:, :, -M1:, :M2].set(jnp.einsum('bixy,ioxy->boxy', x_ft[:, :, -M1:, :M2], w2))
            return jnp.fft.irfft2(out_ft, s=(h, w))
        h = layer_norm(x @ fc0_w + fc0_b, ln0_g, ln0_b)
        h = jnp.transpose(h, (0, 3, 1, 2))
        for i in range(LAYERS):
            w1 = w1r[i] + 1j * w1i[i]
            w2 = w2r[i] + 1j * w2i[i]
            x1 = spectral_conv(h, w1, w2)
            x2 = jnp.einsum('bchw,oc->bohw', h, conv_w[i]) + conv_b[i][None, :, None, None]
            h = x1 + x2
            h = jnp.transpose(h, (0, 2, 3, 1))
            h = layer_norm(h, ln_g[i], ln_b[i])
            if i < LAYERS - 1:
                h = gelu(h)
            h = jnp.transpose(h, (0, 3, 1, 2))
        h = jnp.transpose(h, (0, 2, 3, 1))
        h = gelu(h @ fc1_w + fc1_b)
        h = gelu(h @ fc2_w + fc2_b)
        h = h @ fc3_w + fc3_b
        return h[..., 0]

    def _L0_attn_ref(x, Wqkv, bqkv, W0, b0):
        import jax, jax.numpy as jnp
        import numpy as np
        B, N, D, H = (4, 256, 64, 8)
        b, n, d = x.shape
        h = Wqkv.shape[1] // (3 * d)
        qkv = x @ Wqkv + bqkv
        q, k, v = jnp.reshape(qkv, (3, b, n, d, h))
        score = jnp.einsum('bnqh,btqh->bnth', q, k) * d ** (-0.5)
        attn = jax.nn.softmax(score, axis=1)
        av = jnp.einsum('bnnh,bnqh->bnqh', attn, v)
        out = av.reshape(b, n, d * h) @ W0 + b0
        return out

    def _L0_ffn_ref(x, W1, b1, Wg, bg, Wd, bd):
        import jax, jax.numpy as jnp
        import numpy as np
        C = 64
        HID = 256
        E = 8
        TEMP = 1.0
        orig_shape = x.shape
        xf = x.reshape(-1, orig_shape[-1])
        H = jax.nn.gelu(xf @ W1 + b1, approximate=False)
        probs = jax.nn.softmax((H @ Wg + bg) / TEMP, axis=-1)
        assign = jnp.argmax(probs, axis=-1)
        out = jnp.zeros_like(xf)
        for e in range(Wd.shape[0]):
            y = H @ Wd[e] + bd[e]
            sel = (assign == e)[:, None]
            out = out + jnp.where(sel, probs[:, e:e + 1] * y, 0.0)
        return out.reshape(orig_shape)

    def _L1_attn_ref(embeddings, E, Dx, Dy):
        import jax, jax.numpy as jnp
        import numpy as np
        U_DECAY = 0.97
        X_DECAY = 0.97
        LN_EPS = 1e-05
        L1_EPS = 1e-12

        def _ln(x):
            m = jnp.mean(x, axis=-1, keepdims=True)
            v = jnp.mean((x - m) ** 2, axis=-1, keepdims=True)
            return (x - m) * jax.lax.rsqrt(v + LN_EPS)
        B, T, d = embeddings.shape
        n = E.shape[1]

        def step(carry, v_prev):
            x_state, rho = carry
            x_update = jax.nn.relu(v_prev @ Dx.T)
            x_t = X_DECAY * x_state + x_update
            x_t = x_t / jnp.maximum(jnp.sum(jnp.abs(x_t), axis=-1, keepdims=True), L1_EPS)
            a_star = jnp.einsum('bdn,bn->bd', rho, x_t)
            y_core = _ln(a_star) @ Dy.T
            y_t = jax.nn.relu(y_core) * jax.nn.relu(x_t)
            v_star = _ln(y_t @ E.T)
            rho_t = U_DECAY * rho + _ln(v_prev)[:, :, None] * x_t[:, None, :]
            return ((x_t, rho_t), v_star)
        x0 = jnp.zeros((B, n), dtype=embeddings.dtype)
        rho0 = jnp.zeros((B, d, n), dtype=embeddings.dtype)
        _, vs = jax.lax.scan(step, (x0, rho0), jnp.swapaxes(embeddings, 0, 1))
        return jnp.swapaxes(vs, 0, 1)

    def _L1_ffn_ref(x, Wg, bg, bias, W1, b1, W2, b2):
        import jax, jax.numpy as jnp
        import numpy as np
        D_MODEL = 64
        EXPERT_DIM = 128
        NUM_EXPERTS = 8
        TOP_K = 2
        SEQ_LEN = 512
        BATCH = 2
        x_flat = x.reshape(-1, D_MODEL)
        gate_logits = x_flat @ Wg + bg + bias
        topk_vals, topk_idx = jax.lax.top_k(gate_logits, TOP_K)
        topk_w = jax.nn.softmax(topk_vals, axis=-1)
        combine = (jax.nn.one_hot(topk_idx, NUM_EXPERTS, dtype=x.dtype) * topk_w[..., None]).sum(axis=1)
        h = jax.nn.relu(jnp.einsum('td,edh->teh', x_flat, W1) + b1)
        y = jnp.einsum('teh,ehd->ted', h, W2) + b2
        out = jnp.einsum('ted,te->td', y, combine)
        return out.reshape(x.shape)
    h = _L0_tok_ref(x, L0_tok_fc0_w, L0_tok_fc0_b, L0_tok_ln0_g, L0_tok_ln0_b, L0_tok_w1r, L0_tok_w1i, L0_tok_w2r, L0_tok_w2i, L0_tok_conv_w, L0_tok_conv_b, L0_tok_ln_g, L0_tok_ln_b, L0_tok_fc1_w, L0_tok_fc1_b, L0_tok_fc2_w, L0_tok_fc2_b, L0_tok_fc3_w, L0_tok_fc3_b)
    h = h + _L0_attn_ref(_layernorm(h, axis=-1), L0_attn_Wqkv, L0_attn_bqkv, L0_attn_W0, L0_attn_b0)
    h = h + _L0_ffn_ref(_layernorm(h, axis=-1), L0_ffn_W1, L0_ffn_b1, L0_ffn_Wg, L0_ffn_bg, L0_ffn_Wd, L0_ffn_bd)
    h = h + _L1_attn_ref(_layernorm(h, axis=-1), L1_attn_E, L1_attn_Dx, L1_attn_Dy)
    h = h + _L1_ffn_ref(_layernorm(h, axis=-1), L1_ffn_Wg, L1_ffn_bg, L1_ffn_bias, L1_ffn_W1, L1_ffn_b1, L1_ffn_W2, L1_ffn_b2)
    return h

_drawn_inputs = setup_inputs


def setup_inputs(seed=0):
    import zlib

    import numpy as np

    out = dict(_drawn_inputs(seed))
    spreads = {'L0_tok_fc0_b': (0.0, 0.1),
     'L0_tok_ln0_g': (1.0, 0.2),
     'L0_tok_ln0_b': (0.0, 0.1),
     'L0_tok_conv_b': (0.0, 0.1),
     'L0_tok_ln_g': (1.0, 0.2),
     'L0_tok_ln_b': (0.0, 0.1),
     'L0_tok_fc1_b': (0.0, 0.1),
     'L0_tok_fc2_b': (0.0, 0.1),
     'L0_attn_bqkv': (0.0, 0.8),
     'L0_attn_b0': (0.0, 0.1),
     'L0_ffn_b1': (0.0, 0.401),
     'L0_ffn_bg': (0.0, 0.1),
     'L0_ffn_bd': (0.0, 0.1),
     'L1_ffn_bias': (0.0, 0.5)}
    factors = {'L0_tok_w1r': 8.0,
     'L0_tok_w1i': 8.0,
     'L0_tok_w2r': 8.0,
     'L0_tok_w2i': 8.0,
     'L0_attn_Wqkv': 8.0,
     'L0_attn_W0': 8.0,
     'L0_ffn_W1': 4.115,
     'L0_ffn_Wg': 8.0,
     'L0_ffn_Wd': 2.792,
     'L1_ffn_Wg': 2.764,
     'L1_ffn_bg': 7.73,
     'L1_ffn_W1': 3.487,
     'L1_ffn_b1': 8.0,
     'L1_ffn_W2': 2.919,
     'L1_ffn_b2': 3.722}
    for name, (base, spread) in spreads.items():
        noise = np.random.default_rng([zlib.crc32(name.encode()), seed]).standard_normal(out[name].shape)
        drawn = base * np.exp(spread * noise) if base else spread * noise
        out[name] = jnp.asarray(drawn.astype(out[name].dtype))
    for name, factor in factors.items():
        out[name] = (out[name] * factor).astype(out[name].dtype)
    return out
```

```python
from contextlib import ExitStack

import concourse.bass as bass
from concourse import mybir
import numpy as np

F32 = mybir.dt.float32
ALU = mybir.AluOpType
ACT = mybir.ActivationFunctionType
AX = mybir.AxisListType

IMGS, S, CH, CIN = 64, 64, 32, 3
LAYERS, M1, M2 = 4, 12, 12
GROUP, UNITS = 16, 2
GROUPS = IMGS // GROUP
UIMG = GROUP // UNITS
NA, NB = 4, 2
KX = 2 * M1
KP = M2 // 2
STAGES = LAYERS + 1
NCH = S // 4
UCOLS = S * NA * CH
EPS = 1e-5

AX_EMBED, AX_ROWS, AX_A, AX_B, AX_MIX, AX_C = 1, 8, 8, 2, 3, 8
AX_FWD = AX_ROWS + AX_A + AX_B + AX_MIX
AX_MLP = 1
AX_STAGE0 = UNITS * (AX_EMBED + AX_FWD)
AX_LAYER = UNITS * (AX_C + AX_FWD)
AX_LAST = UNITS * AX_C
AX_GROUP = AX_STAGE0 + (LAYERS - 1) * AX_LAYER + AX_LAST + UNITS * AX_MLP

CHUNKS_GROUP = STAGES * UNITS * NCH
MLP_BLOCKS = NB * S // 8
FC1_GROUP = UNITS * MLP_BLOCKS * NA
FC2_GROUP = FC1_GROUP // 2
FC1, FC2 = 128, 64


def dft_tables():
    n = np.arange(S)
    ky = np.arange(M2)
    kx = np.concatenate([np.arange(M1), np.arange(S - M1, S)])
    w_ang = 2 * np.pi * np.outer(n, ky) / S
    r_ang = 2 * np.pi * np.outer(n, kx) / S
    fwd_w = np.zeros((NB, S, NB, 2, M2, 2))
    cos_r = np.zeros((2, S, 2, KX))
    sin_r = np.zeros((2, S, 2, KX))
    for i in range(2):
        fwd_w[i, :, i, 0, :, 0] = np.cos(w_ang)
        fwd_w[i, :, i, 0, :, 1] = -np.sin(w_ang)
        fwd_w[i, :, i, 1, :, 0] = -np.sin(w_ang)
        fwd_w[i, :, i, 1, :, 1] = -np.cos(w_ang)
        cos_r[i, :, i] = np.cos(r_ang)
        sin_r[i, :, i] = np.sin(r_ang)
    weight = np.where(ky == 0, 1.0, 2.0)[:, None] / (S * S)
    inv_w = np.zeros((M2, 2, 4, 4, S))
    for i in range(4):
        inv_w[:, 0, i, i] = weight * np.cos(w_ang.T)
        inv_w[:, 1, i, i] = weight * np.sin(w_ang.T)
    inv_r = np.zeros((2, 2, NB, M1, S, NB))
    for i in range(NB):
        inv_r[0, :, i, :, :, i] = np.cos(r_ang.T).reshape(2, M1, S)
        inv_r[1, :, i, :, :, i] = -np.sin(r_ang.T).reshape(2, M1, S)
    inv_r = np.concatenate([inv_r.reshape(4 * KX, 128), np.ones((1, 128))])
    ident = np.eye(128)
    center = np.eye(CH) - 1.0 / CH
    spread = np.zeros((4, 97))
    mask = np.zeros((97, 8, NA))
    for a in range(NA):
        for w in range(8):
            for c in range(CIN):
                spread[c, a * 24 + w * 3 + c] = 1
                mask[a * 24 + w * 3 + c, w, a] = 1
    spread[3, 96] = 1
    mask[96] = 1
    f = np.float32
    return {
        "t_fwd_w": fwd_w.reshape(128, 96).astype(f), "t_cos_r": cos_r.reshape(128, 48).astype(f),
        "t_sin_r": sin_r.reshape(128, 48).astype(f), "t_inv_w": inv_w.reshape(96, 256).astype(f),
        "t_inv_r": inv_r.astype(f), "t_ident": ident.astype(f), "t_center": center.astype(f),
        "t_spread": spread.astype(f), "t_mask": mask.reshape(97, 32).astype(f),
    }


def tokenizer(nc, t, tok, named):
    ctx = ExitStack()

    def sb(name, shape):
        return ctx.enter_context(nc.sbuf_tensor(name, shape, F32))

    def sem(name):
        return named.enter_context(nc.semaphore(name))

    with ctx:
        mix_scratch = nc.dram_tensor("mix_scratch", (LAYERS, 128, 2 * 2 * M1 * KP * CH), F32, kind="Internal").ap()
        bias_scratch = nc.dram_tensor("bias_scratch", (LAYERS, 16 * NA * CH), F32, kind="Internal").ap()
        embw_scratch = nc.dram_tensor("embw_scratch", (97, 8 * NA * CH), F32, kind="Internal").ap()
        y_scratch = nc.dram_tensor("y_scratch", (UNITS, 2, M2 * 2 * CH * KX * UIMG), F32, kind="Internal").ap()

        h = sb("h", [128, UNITS * NB * S * S])
        pix = sb("pix", [128, UCOLS])
        mixw = sb("mixw", [128, 2 * 2 * M1 * KP * CH])
        t_w = sb("t_w", [128, 2 * NB * 2 * M2 * 2 * CH])
        XC = KP * KX * 2 * UIMG
        xs = sb("xs", [128, XC + 2 * 2 * UIMG])
        HN = NB * M1 * NA
        ys = t_w[:, 1024:1024 + M2 * HN]
        yn = t_w[:, 1024 + M2 * HN:1024 + 2 * M2 * HN]
        YC = 2 * 8 * KX * UIMG
        yd = sb("yd", [128, UNITS * YC])
        sq = sb("sq", [128, 2, 512])
        xn = sb("xn", [128, 2, 512])
        ssum = sb("ssum", [128, 4, 16])
        var = sb("var", [128, 4, 16])
        rstd = sb("rstd", [128, 4, 16])
        mhalf = sb("mhalf", [128, 16])
        eps = sb("eps", [128, 16])
        fwd_w = sb("fwd_w", [128, 96])
        cos_r = sb("cos_r", [128, 96])
        sin_r = sb("sin_r", [128, 96])
        inv_w = sb("inv_w", [96, 256])
        inv_r = sb("inv_r", [97, 128])
        ident = sb("ident", [128, 128])
        convw = sb("convw", [128, LAYERS, 128])
        gb = sb("gb", [128, 2, STAGES])
        f1w = sb("f1w", [128, NA, FC1])
        f2w = sb("f2w", [128, FC2])
        f3w = sb("f3w", [128, 2])
        fb = sb("fb", [128, 3])

        def xb_of(u):
            return yd[:, u * YC:u * YC + NA * S * CIN]

        def embw_of(u):
            return yd[0:97, u * YC + 2048:u * YC + 3072]

        def xt_of(u):
            return yd[0:97, u * YC + 1024:u * YC + 2048]

        main = [ctx.enter_context(nc.psum_tensor(f"main{i}", [128, 512], F32)) for i in range(4)]
        tp = [ctx.enter_context(nc.psum_tensor(f"tp{i}", [128, 512], F32)) for i in range(2)]
        aux = [ctx.enter_context(nc.psum_tensor(f"aux{i}", [128, 512], F32)) for i in range(2)]

        p_sum, p_cent, p_neg, p_store = (sem(n) for n in ("p_sum", "p_cent", "p_neg", "p_store"))
        p_raw = sem("p_raw")
        p_zero, p_small, p_pe, p_done, p_bias, p_bstore = (
            sem(n) for n in ("p_zero", "p_small", "p_pe", "p_done", "p_bias", "p_bstore"))
        NRAW = CH * M1 * M2
        raw = h[:, 0:2 * NRAW].rearrange("p (v n) -> p v n", v=2)
        rsum = t_w[:, 0:2 * M1 * M2].rearrange("p (v n) -> p v n", v=2)
        cent = mixw[:, :].rearrange("p (k x y s o) -> p k x y s o", k=2, x=M1, y=KP, s=2)
        cload = xs[0:CH, 0:LAYERS * 128]
        cmat = xs[0:CH, 1024:1056]
        braw = ys[0:1, 0:LAYERS * CH]
        bsum = ys[0:1, 256:256 + LAYERS]
        bcen = ys[0:1, 512:512 + LAYERS * CH]
        eraw = sq[0:4, 0, 0:CH]
        esum = sq[0:4, 0, 64:65]
        ecen = sq[0:4, 0, 128:128 + CH]
        spread = sq[0:4, 0, 256:256 + 97]
        mask = sq[0:97, 1, 0:32]
        n_small = 0
        with nc.Block() as block:
            @block.sync
            def _(sp):
                sp.wait_ge(p_zero, 5)
                loads = [(fwd_w[:, :], t["t_fwd_w"]), (cos_r[:, 0:48], t["t_cos_r"]), (sin_r[:, 0:48], t["t_sin_r"]),
                         (inv_w[:, :], t["t_inv_w"]), (inv_r[:, :], t["t_inv_r"]), (ident[:, :], t["t_ident"]),
                         (cmat, t["t_center"]), (spread, t["t_spread"]), (mask, t["t_mask"]),
                         (eraw[0:CIN, :], t["L0_tok_fc0_w"]),
                         (eraw[CIN:4, :], t["L0_tok_fc0_b"].rearrange("(a n) -> a n", a=1)),
                         (braw, t["L0_tok_conv_b"].rearrange("(x l) o -> x (l o)", x=1)),
                         (f2w[:, :], t["L0_tok_fc2_w"]),
                         (fb[:, 0:1], t["L0_tok_fc1_b"].rearrange("(n a) -> n a", a=1)),
                         (fb[:, 2:3], t["L0_tok_fc3_b"].rearrange("(n a) -> n a", a=1).to_broadcast([128, 1]))]
                for a in range(NA):
                    rows = slice(32 * a, 32 * a + 32)
                    loads.append((cload.rearrange("o (l a c) -> o l a c", l=LAYERS, a=NA)[:, :, a, :],
                                  t["L0_tok_conv_w"].rearrange("l o c -> o l c")))
                    loads.append((gb[rows, 0, 0:1], t["L0_tok_ln0_g"].rearrange("(n a) -> n a", a=1)))
                    loads.append((gb[rows, 1, 0:1], t["L0_tok_ln0_b"].rearrange("(n a) -> n a", a=1)))
                    for l in range(LAYERS):
                        loads.append((gb[rows, 0, l + 1:l + 2], t["L0_tok_ln_g"][l, :].rearrange("(n a) -> n a", a=1)))
                        loads.append((gb[rows, 1, l + 1:l + 2], t["L0_tok_ln_b"][l, :].rearrange("(n a) -> n a", a=1)))
                    loads.append((f1w[rows, a, :], t["L0_tok_fc1_w"]))
                for i in range(2):
                    rows = slice(64 * i, 64 * i + 64)
                    loads.append((f3w[rows, i:i + 1], t["L0_tok_fc3_w"]))
                    loads.append((fb[rows, 1:2], t["L0_tok_fc2_b"].rearrange("(n a) -> n a", a=1)))
                for dst, src in loads:
                    sp.dma_start(dst, src).then_inc(p_small, 16)
                assert len(loads) == N_SMALL
                sp.wait_ge(p_bias, 2)
                for l in range(LAYERS):
                    sp.dma_start(bias_scratch[l, :].rearrange("(x r o) -> x r o", x=1, o=CH),
                                 bcen[:, l * CH:(l + 1) * CH].unsqueeze(1).to_broadcast([1, 16 * NA, CH])).then_inc(p_bstore, 16)
                sp.wait_ge(p_done, 3)
                sp.dma_start(embw_scratch, embw_of(0)).then_inc(p_bstore, 16)
                sp.wait_ge(p_bstore, 16 * (LAYERS + 1))

            @block.gpsimd
            def _(pool):
                for l in range(LAYERS):
                    if l >= 1:
                        pool.wait_ge(p_cent, 4 * l)
                    for q, names in enumerate((("w1r", "w1i"), ("w1i", "w1r"), ("w2r", "w2i"), ("w2i", "w2r"))):
                        for v in range(2):
                            pool.dma_start(raw[32 * q:32 * q + 32, v, :],
                                           t["L0_tok_" + names[v]][l].rearrange("i o x y -> i (o x y)")).then_inc(p_raw, 16)
                    pool.wait_ge(p_neg, 2 * (l + 1))
                    dst = mix_scratch[l].rearrange("(k q) (f n) -> q k f n", k=2, f=2)
                    for half in range(2):
                        pool.dma_start(dst[:, :, half, :],
                                       mixw[64 * half:64 * half + 64, :].rearrange("q (k n) -> q k n", k=2)).then_inc(p_store, 16)
                    pool.wait_ge(p_store, 32 * (l + 1))

            @block.vector
            def _(dve):
                dve.memset(convw[:, :, :], 0.0).then_inc(p_zero, 1)
                dve.memset(f1w[:, :, :], 0.0).then_inc(p_zero, 1)
                dve.memset(f3w[:, :], 0.0).then_inc(p_zero, 1)
                dve.memset(cos_r[:, 48:96], 0.0).then_inc(p_zero, 1)
                dve.memset(sin_r[:, 48:96], 0.0).then_inc(p_zero, 1)
                dve.memset(mhalf[:, :], -0.5)
                dve.memset(eps[:, :], EPS)
                for u in range(UNITS):
                    dve.memset(yd[96:97, u * YC + 1024:u * YC + 2048], 1.0)
                for l in range(LAYERS):
                    dve.wait_ge(p_raw, 128 * (l + 1))
                    for v in range(2):
                        dve.tensor_reduce(rsum[:, v, :], raw[:, v, :].rearrange("p (o n) -> p n o", o=CH), AX.X,
                                          ALU.add).then_inc(p_sum, 1)
                    dve.wait_ge(p_sum, 2 * (l + 1))
                    if l >= 1:
                        dve.wait_ge(p_store, 32 * l)
                    for v in range(2):
                        for k in range(2):
                            dve.scalar_tensor_tensor(
                                out=cent[:, k, :, :, v, :],
                                in0=rsum[:, v, :].rearrange("p (x y k) -> p x y k", x=M1, k=2)[:, :, :, k].unsqueeze(3).to_broadcast([128, M1, KP, CH]),
                                scalar=-1.0 / CH,
                                in1=raw[:, v, :].rearrange("p (o x y k) -> p x y o k", o=CH, x=M1, k=2)[:, :, :, :, k],
                                op0=ALU.mult, op1=ALU.add).then_inc(p_cent, 1)
                dve.wait_ge(p_small, 16 * N_SMALL)
                dve.tensor_reduce(bsum, braw.rearrange("p (l o) -> p l o", l=LAYERS), AX.X, ALU.add).then_inc(p_bias, 1)
                dve.wait_ge(p_bias, 1)
                dve.scalar_tensor_tensor(out=bcen.rearrange("p (l o) -> p l o", l=LAYERS),
                                         in0=bsum.unsqueeze(2).to_broadcast([1, LAYERS, CH]), scalar=-1.0 / CH,
                                         in1=braw.rearrange("p (l o) -> p l o", l=LAYERS),
                                         op0=ALU.mult, op1=ALU.add).then_inc(p_bias, 1)
                dve.tensor_reduce(esum, eraw, AX.X, ALU.add).then_inc(p_done, 1)
                dve.wait_ge(p_done, 1)
                dve.scalar_tensor_tensor(out=ecen, in0=esum.to_broadcast([4, CH]), scalar=-1.0 / CH, in1=eraw,
                                         op0=ALU.mult, op1=ALU.add).then_inc(p_done, 1)
                dve.wait_ge(p_pe, 1)
                dve.tensor_tensor(embw_of(0).rearrange("p (m o) -> p m o", o=CH),
                                  mask.unsqueeze(2).to_broadcast([97, 32, CH]),
                                  aux[0][0:97, 0:CH].unsqueeze(1).to_broadcast([97, 32, CH]), ALU.mult).then_inc(p_done, 1)
                dve.wait_ge(p_pe, 2)
                for l in range(LAYERS):
                    for a in range(NA):
                        dve.tensor_copy(convw[32 * a:32 * a + 32, l, 32 * a:32 * a + 32],
                                        aux[1][32 * a:32 * a + 32, 32 * l:32 * l + 32])

            @block.scalar
            def _(act):
                for l in range(LAYERS):
                    act.wait_ge(p_cent, 4 * (l + 1))
                    for q in (32, 96):
                        v = mixw[q:q + 32, :].rearrange("p (n s o) -> p n s o", s=2, o=CH)[:, :, 0, :]
                        act.mul(v, v, -1.0).then_inc(p_neg, 1)

            @block.tensor
            def _(pe):
                pe.wait_ge(p_small, 16 * N_SMALL)
                pe.wait_ge(p_done, 2)
                pe.matmul(aux[0][0:97, 0:CH], spread, ecen, start=True, stop=True).then_inc(p_pe, 1)
                for l in range(LAYERS):
                    mm = pe.matmul(aux[1][:, 32 * l:32 * l + 32], cload[:, 128 * l:128 * l + 128], cmat,
                                   start=True, stop=True)
                mm.then_inc(p_pe, 1)

        main_full, main_free, sq_full, red_done, var_done, rstd_done, tp_full, tp_free = (
            sem(n) for n in ("main_full", "main_free", "sq_full", "red_done", "var_done", "rstd_done", "tp_full", "tp_free"))
        aux_full = [sem(f"aux_full{i}") for i in range(2)]
        aux_free = [sem(f"aux_free{i}") for i in range(2)]
        bias_in, mixw_in, xs_zero, y_ready, y_stored = (
            sem(n) for n in ("bias_in", "mixw_in", "xs_zero", "y_ready", "y_stored"))
        x_in = [sem(f"x_in{u}") for u in range(UNITS)]
        yd_in = [sem(f"yd_in{u}") for u in range(UNITS)]
        fc1_full, g1_done, fc2_full, g2_done, tok_out = (
            sem(n) for n in ("fc1_full", "g1_done", "fc2_full", "g2_done", "tok_out"))

        hv = h[:, :].rearrange("p (u n w) -> p u n w", u=UNITS, w=S)
        pv = pix[:, :].rearrange("p (c a r) -> p c a r", r=S, a=NA)
        qv = pix[0:97, :].rearrange("p (w a c) -> p w a c", w=S, a=NA)
        tv = t_w[:, :].rearrange("p (j b v k s c) -> p j b v k s c", j=2, b=NB, v=2, k=M2, s=2)
        mv = mixw[:, :].rearrange("p (x y n) -> p x y n", x=KX, y=KP)
        xv = xs[:, 0:XC].rearrange("p (y x k b a) -> p y x k b a", y=KP, x=KX, k=2, b=NB)
        yv = ys.rearrange("p (y m x a) -> p y m x a", y=KP, m=2 * NB, x=M1)
        ydv = yd[0:96, :].rearrange("p (u o n a) -> p u o n a", u=UNITS, o=8, a=NA)
        g1 = pix[:, 0:4 * 512].rearrange("p (j n) -> p j n", j=4)
        g2 = pix[:, 4 * 512:8 * 512].rearrange("p (j n) -> p j n", j=4)
        tokt = pix[:, 4096:4352]
        tokb = pix[:, 4608:4864]

        def base_of(g, s, u, l=None):
            if l is not None:
                return (g * CHUNKS_GROUP + l * (UNITS * NCH) + (UNITS + u) * NCH,
                        g * AX_GROUP + l * AX_LAYER + (AX_STAGE0 + u * (AX_LAYER // 2)))
            chunks = g * CHUNKS_GROUP + (s * UNITS + u) * NCH
            if s == 0:
                return chunks, g * AX_GROUP + u * (AX_STAGE0 // 2)
            done = AX_STAGE0 + (s - 1) * AX_LAYER
            return chunks, g * AX_GROUP + (done + u * (AX_C if s == LAYERS else AX_LAYER // 2))

        def after(n, c, depth):
            return n + max(0, c - depth + 1)

        def pe_aux(pe, j, n):
            pe.wait_ge(aux_free[j], n)

        def pe_embed(pe, g, u):
            _, n = base_of(g, 0, u)
            pe.wait_ge(x_in[u], (g + 1) * ((UIMG + 1) * 16))
            for j in range(2):
                pe_aux(pe, j, n)
                for i in range(4):
                    o = (4 * j + i) * 96
                    mm = pe.transpose(aux[j][0:96, 128 * i:128 * i + 128], xb_of(u)[:, o:o + 96], ident[:, :])
                mm.then_inc(aux_full[j], 1)
            for j in range(2):
                pe.wait_ge(aux_free[j], n + 1)

        def pe_inverse(pe, g, s, u, l):
            _, n = base_of(g, s, u, l)
            stage = l if l is not None else s - 1
            pe.wait_ge(yd_in[u], (g * LAYERS + stage + 1) * 32)
            for k in range(2 * AX_C):
                j, a, o = k % 2, k // 4, 2 * (k % 4)
                pe_aux(pe, j, n + k // 2)
                for i in range(2):
                    mm = pe.matmul(aux[j][0:96, 256 * i:256 * i + 256], ydv[:, u, o + i, :, a],
                                   inv_w[:, :], start=True, stop=True)
                mm.then_inc(aux_full[j], 1)
            for j in range(2):
                pe.wait_ge(aux_free[j], n + AX_C)
            pe.wait_ge(bias_in, (g * (LAYERS * UNITS) + stage * UNITS + (u + 1)) * 16)

        def pe_main(pe, g, s, u, l):
            m, _ = base_of(g, s, u, l)
            layer = l if l is not None else s - 1
            lag = 3
            for c in range(NCH + lag):
                if c < NCH:
                    bank = main[c % 4]
                    pe.wait_ge(main_free, after(m, c, 4))
                    if s == 0:
                        mm = pe.matmul(bank[:, :], xt_of(u)[:, 128 * (c // 2):128 * (c // 2) + 128],
                                       embw_of(u)[:, 512 * (c % 2):512 * (c % 2) + 512], start=True, stop=True)
                    else:
                        pe.matmul(bank[:, :], inv_r[:, :], pix[0:97, 512 * c:512 * c + 512], start=True, stop=False)
                        for i in range(4):
                            mm = pe.matmul(bank[:, 128 * i:128 * i + 128], hv[:, u, :, 4 * c + i],
                                           convw[:, layer, :] if l is None else convw[:, bass.ds(layer, 1), :], start=False, stop=(i == 3))
                    mm.then_inc(main_full, 1)
                if c >= lag:
                    d = c - lag
                    pe.wait_ge(main_free, m + d + 1)
                    pe.wait_ge(tp_free, after(m, d, 2))
                    for i in range(4):
                        mm = pe.transpose(tp[d % 2][:, 128 * i:128 * i + 128], xn[:, d % 2, 128 * i:128 * i + 128],
                                          ident[:, :])
                    mm.then_inc(tp_full, 1)

        def pe_forward(pe, g, s, u, l):
            m, n = base_of(g, s, u, l)
            n = n + (AX_EMBED if s == 0 else AX_C)
            pe.wait_ge(tp_free, m + NCH)
            for k in range(2 * AX_ROWS):
                j = k % 2
                pe_aux(pe, j, n + k // 2)
                for i in range(4):
                    mm = pe.transpose(aux[j][:, 128 * i:128 * i + 128], h[:, (u * S + 4 * k + i) * 128:(u * S + 4 * k + i) * 128 + 128],
                                      ident[:, :])
                mm.then_inc(aux_full[j], 1)
            n = n + AX_ROWS
            for j in range(2):
                pe.wait_ge(aux_free[j], n)
            for k in range(2 * AX_A):
                j, ap, c0 = k % 2, k // 8, 4 * (k % 8)
                pe_aux(pe, j, n + k // 2)
                for i in range(4):
                    mm = pe.matmul(aux[j][:, 96 * i:96 * i + 96],
                                   pv[:, c0 + i, 2 * ap:2 * ap + 2, :].rearrange("p a r -> p (a r)"),
                                   fwd_w[:, :], start=True, stop=True)
                mm.then_inc(aux_full[j], 1)
            n = n + AX_A
            for j in range(2):
                pe.wait_ge(aux_free[j], n)
            if u == 0:
                pe.wait_ge(mixw_in, (g * LAYERS + (0 if s == 0 else (l + 1)) + 1) * 16)
            for k in range(2 * AX_B):
                j, ap, b = k % 2, k // 2, k % 2
                pe_aux(pe, j, n + k // 2)
                for y in range(KP):
                    o = aux[j][:, 48 * y:48 * y + 96]
                    for v, table in enumerate((cos_r, sin_r)):
                        mm = pe.matmul(o, tv[:, ap, b, v, 2 * y:2 * y + 2].rearrange("p k s c -> p (k s c)"), table[:, :],
                                       start=(v == 0), stop=(v == 1), skip_group_check=True)
                mm.then_inc(aux_full[j], 1)
            n = n + AX_B
            for j in range(2):
                pe.wait_ge(aux_free[j], n)
            for y in range(2 * AX_MIX):
                j = y % 2
                pe_aux(pe, j, n + y // 2)
                for x in range(M1):
                    for half in range(2):
                        at = ((y * KX + half * M1 + x) * 2) * UIMG
                        mm = pe.matmul(aux[j][64 * half:64 * half + 64, 16 * x:16 * x + 48],
                                       mv[:, half * M1 + x, y, :], xs[:, at:at + 48],
                                       start=True, stop=True, skip_group_check=True)
                mm.then_inc(aux_full[j], 1)

        def pe_mlp(pe, g, u):
            n = g * AX_GROUP + (AX_GROUP - UNITS * AX_MLP + u)
            f1 = g * FC1_GROUP + u * (FC1_GROUP // 2)
            f2 = g * FC2_GROUP + u * (FC2_GROUP // 2)
            if u == 0:
                pe.wait_ge(main_free, (g + 1) * CHUNKS_GROUP)
                pe.wait_ge(tp_free, (g + 1) * CHUNKS_GROUP)
            pe_aux(pe, 0, n)
            total = MLP_BLOCKS * NA
            hb = h[:, :].rearrange("p (u k n) -> p u k n", u=UNITS, n=512)
            for i in range(total + 6):
                if i < total:
                    k, a = i // NA, i % NA
                    pe.wait_ge(g1_done, after(f1, i, 4))
                    pe.matmul(main[i % 4][:, :], f1w[:, a, :], hb[:, u, k, :], start=True, stop=True).then_inc(fc1_full, 1)
                if 2 <= i < total + 2:
                    d = i - 2
                    pe.wait_ge(g1_done, f1 + d + 1)
                    if d % 2 == 0:
                        pe.wait_ge(g2_done, after(f2, d // 2, 2))
                    mm = pe.matmul(tp[d // 2 % 2][64 * (d % 2):64 * (d % 2) + 64, :], f2w[:, :], g1[:, d % 4, :],
                                   start=True, stop=True)
                    if d % 2:
                        mm.then_inc(fc2_full, 1)
                if i >= 6 and i % 2 == 0:
                    d = (i - 6) // 2
                    pe.wait_ge(g2_done, f2 + d + 1)
                    for q in range(4):
                        k = d // 2
                        col = 128 * (d % 2) + 4 * k + q
                        mm = pe.matmul(aux[0][:, col:col + 65:64], g2[:, d % 4, 128 * q:128 * q + 128], f3w[:, :],
                                       start=True, stop=True)
            mm.then_inc(aux_full[0], 1)
            pe_aux(pe, 1, n)
            pe.wait_ge(aux_free[0], n + 1)
            for i in range(2):
                mm = pe.transpose(aux[1][:, 128 * i:128 * i + 128], tokt[:, 128 * i:128 * i + 128], ident[:, :])
            mm.then_inc(aux_full[1], 1)

        def copy(eng, j, out, in_):
            return eng.tensor_copy(out, in_) if j == 0 else eng.copy(out, in_)

        def drain_embed(eng, j, g, u):
            _, n = base_of(g, 0, u)
            eng.wait_ge(aux_full[j], n + 1)
            copy(eng, j, xt_of(u)[0:96, 512 * j:512 * j + 512], aux[j][0:96, :]).then_inc(aux_free[j], 1)

        def drain_inverse(eng, j, g, s, u, l):
            _, n = base_of(g, s, u, l)
            for k in range(j, 2 * AX_C, 2):
                a, o = k // 4, 2 * (k % 4)
                eng.wait_ge(aux_full[j], n + (k // 2 + 1))
                out = qv[0:96, :, a, :].rearrange("p w (d e) -> p e d w", d=4)[:, o:o + 2]
                copy(eng, j, out, aux[j][0:96, :].rearrange("p (e d w) -> p e d w", e=2, d=4)).then_inc(aux_free[j], 1)

        def drain_forward(eng, j, g, s, u, l):
            _, n = base_of(g, s, u, l)
            n = n + (AX_EMBED if s == 0 else AX_C)
            fwd = (g * (LAYERS * UNITS) + (0 if s == 0 else l * UNITS + UNITS) + u)
            for k in range(j, 2 * AX_ROWS, 2):
                eng.wait_ge(aux_full[j], n + (k // 2 + 1))
                copy(eng, j, pv[:, :, :, 4 * k:4 * k + 4].rearrange("p c a r -> p a c r"),
                     aux[j][:, :].rearrange("p (r a c) -> p a c r", r=4, a=NA)).then_inc(aux_free[j], 1)
            n = n + AX_ROWS
            eng.wait_ge(y_stored, fwd * 128)
            for k in range(j, 2 * AX_A, 2):
                ap, c0 = k // 8, 4 * (k % 8)
                eng.wait_ge(aux_full[j], n + (k // 2 + 1))
                out = tv[:, ap, :, :, :, :, c0:c0 + 4].rearrange("p b v k s c -> p (b v k s) c")
                copy(eng, j, out, aux[j][:, 0:384].rearrange("p (c n) -> p n c", c=4)).then_inc(aux_free[j], 1)
            n = n + AX_A
            for k in range(j, 2 * AX_B, 2):
                ap, b = k // 2, k % 2
                eng.wait_ge(aux_full[j], n + (k // 2 + 1))
                for ky in range(2):
                    rows = slice(64 * ky, 64 * ky + 64)
                    out = xv[rows, :, :, ky, b, 2 * ap:2 * ap + 2].rearrange("p y x a -> p y a x")
                    ins = copy(eng, j, out, aux[j][rows, 0:288].rearrange("p (y a x) -> p y a x", y=KP, a=2))
                ins.then_inc(aux_free[j], 1)
            n = n + AX_B
            for k in range(j, 2 * AX_MIX, 2):
                eng.wait_ge(aux_full[j], n + (k // 2 + 1))
                copy(eng, j, yv[:, k], aux[j][:, 0:192].rearrange("p (x m a) -> p m x a", m=2 * NB, a=NA)).then_inc(aux_free[j], 1)
            if j == 0:
                eng.wait_ge(aux_free[0], n + AX_MIX)
                eng.wait_ge(aux_free[1], n + AX_MIX)
                eng.tensor_scalar(yn, ys, -1.0, None, ALU.mult).then_inc(y_ready, 1)

        def dve_main(dve, g, s, u, l):
            m, _ = base_of(g, s, u, l)
            lag = 2
            for c in range(NCH + lag):
                if c < NCH:
                    dve.wait_ge(sq_full, m + c + 1)
                    dve.wait_ge(rstd_done, after(m, c, 4))
                    dve.tensor_reduce(ssum[:, c % 4, :], sq[:, c % 2, :].rearrange("p (n c) -> p n c", c=CH), AX.X,
                                      ALU.add).then_inc(red_done, 1)
                if c >= lag:
                    d = c - lag
                    dve.wait_ge(rstd_done, m + d + 1)
                    dve.wait_ge(tp_full, after(m, d, 2))
                    dve.tensor_tensor(xn[:, d % 2, :].rearrange("p (n c) -> p n c", c=CH),
                                      main[d % 4][:, :].rearrange("p (n c) -> p n c", c=CH),
                                      rstd[:, d % 4, :].unsqueeze(2).to_broadcast([128, 16, CH]),
                                      ALU.mult).then_inc(main_free, 1)

        def act_main(act, g, s, u, l):
            m, _ = base_of(g, s, u, l)
            stage = l + 1 if l is not None else s
            fn = ACT.Identity if s in (0, LAYERS) else ACT.Gelu
            lag = 3
            for c in range(NCH + lag):
                if c < NCH:
                    act.wait_ge(main_full, m + c + 1)
                    act.wait_ge(red_done, after(m, c, 2))
                    act.activation(sq[:, c % 2, :], main[c % 4][:, :], ACT.Square, scale=CH ** -0.5).then_inc(sq_full, 1)
                if c >= lag:
                    d = c - lag
                    act.wait_ge(p_small, 16 * N_SMALL)
                    act.wait_ge(tp_full, m + d + 1)
                    act.activation(hv[:, u, :, 4 * d:4 * d + 4].rearrange("p n w -> p w n"),
                                   tp[d % 2][:, :].rearrange("p (w n) -> p w n", w=4), fn,
                                   bias=gb[:, 1, stage:stage + 1] if l is None else gb[:, 1, bass.ds(stage, 1)],
                                   scale=gb[:, 0, stage:stage + 1] if l is None else gb[:, 0, bass.ds(stage, 1)]).then_inc(tp_free, 1)

        def pool_main(pool, g, s, u, l):
            m, _ = base_of(g, s, u, l)
            for c in range(NCH):
                pool.wait_ge(red_done, m + c + 1)
                pool.tensor_tensor(var[:, c % 4, :], ssum[:, c % 4, :], eps[:, :], ALU.add).then_inc(var_done, 1)
                pool.wait_ge(var_done, m + c + 1)
                pool.wait_ge(main_free, after(m, c, 4))
                pool.tensor_tensor(rstd[:, c % 4, :], var[:, c % 4, :], mhalf[:, :], ALU.pow).then_inc(rstd_done, 1)

        def act_mlp(act, g, u):
            n = g * AX_GROUP + (AX_GROUP - UNITS * AX_MLP + u)
            f1 = g * FC1_GROUP + u * (FC1_GROUP // 2)
            f2 = g * FC2_GROUP + u * (FC2_GROUP // 2)
            for i in range(MLP_BLOCKS * NA + 3):
                if i < MLP_BLOCKS * NA:
                    act.wait_ge(fc1_full, f1 + i + 1)
                    if i >= 4:
                        act.wait_ge(fc2_full, f2 + (i - 2) // 2)
                    act.activation(g1[:, i % 4, :], main[i % 4][:, :], ACT.Gelu, bias=fb[:, 0:1]).then_inc(g1_done, 1)
                if i >= 3 and i % 2 == 1:
                    d = (i - 3) // 2
                    act.wait_ge(fc2_full, f2 + d + 1)
                    if d >= 4:
                        act.wait_ge(fc1_full, f1 + min(MLP_BLOCKS * NA, 2 * (d - 4) + 8))
                    act.activation(g2[:, d % 4, :], tp[d % 2][:, :], ACT.Gelu, bias=fb[:, 1:2]).then_inc(g2_done, 1)
            act.wait_ge(aux_full[1], n + 1)
            act.wait_ge(tok_out, (g * UNITS + u) * 32)
            act.copy(tokb, aux[1][:, 0:256]).then_inc(aux_free[1], 1)

        def dve_mlp(dve, g, u):
            n = g * AX_GROUP + (AX_GROUP - UNITS * AX_MLP + u)
            dve.wait_ge(aux_full[0], n + 1)
            dve.tensor_scalar(tokt, aux[0][:, 0:256], fb[:, 2:3], None, ALU.add).then_inc(aux_free[0], 1)

        def sp_x(sp, g, u):
            for b in range(NB):
                for a in range(NA):
                    img = g * GROUP + (u * UIMG + b * NA + a)
                    sp.dma_start(xb_of(u)[b:128:2, :].rearrange("r (k a n) -> r a k n", k=8, a=NA)[:, a],
                                 t["x"][bass.ds(img, 1)].rearrange("a r (k w) c -> r (a k) (w c)", k=8)).then_inc(x_in[u], 16)

            sp.dma_start(embw_of(u), embw_scratch).then_inc(x_in[u], 16)

        def sp_bias(sp, g, s, u, l):
            _, n = base_of(g, s, u, l)
            layer = l if l is not None else s - 1
            if s == LAYERS and u == 1:
                sp.wait_ge(main_full, g * CHUNKS_GROUP + (LAYERS * UNITS + 1) * NCH)
            else:
                sp.wait_ge(aux_full[1], n - (AX_B + AX_MIX))
            sp.dma_start(pix[96:97, :].rearrange("p (k n) -> p k n", k=4),
                         bias_scratch[bass.ds(layer, 1), :].unsqueeze(1).to_broadcast([1, 4, 16 * NA * CH])).then_inc(bias_in, 16)

        def sp_spectrum(sp, g, s, u, l):
            fwd = (g * (LAYERS * UNITS) + (0 if s == 0 else l * UNITS + UNITS) + u)
            sp.wait_ge(y_ready, fwd + 1)
            for half in range(2):
                for ro, ri, src in ((0, 0, ys), (0, 1, yn), (1, 0, ys), (1, 1, ys)):
                    part = ri if ro == 0 else 1 - ri
                    rows = 64 * half + 32 * part
                    dst = y_scratch[u, ro].rearrange("(y r o f n) -> o y r f n", y=M2, r=2, o=CH, f=2)[:, :, ri, half, :]
                    sp.dma_start(dst, src[rows:rows + 32, :].rearrange("o (y n) -> o y n", y=M2)).then_inc(y_stored, 16)
            sp.wait_ge(y_stored, fwd * 128 + 128)
            for ro in range(2):
                sp.dma_start(yd[0:96, u * YC:(u + 1) * YC].rearrange("p (e s n) -> p e s n", e=8, s=2)[:, :, ro],
                             y_scratch[u, ro].rearrange("(p e n) -> p e n", p=96, e=8)).then_inc(yd_in[u], 16)

        def sp_mixw(sp, layer):
            sp.dma_start(mixw[:, :], mix_scratch[bass.ds(layer, 1)].rearrange("a p n -> (a p) n")).then_inc(mixw_in, 16)

        def sp_tok(sp, g, u):
            n = g * AX_GROUP + (AX_GROUP - UNITS * AX_MLP + u)
            sp.wait_ge(aux_free[1], n + 1)
            for i in range(2):
                img = g * GROUP + (u * UIMG)
                sp.dma_start(tok[bass.ds(img, UIMG)].rearrange("(b i a) r w -> i (a r) b w", b=NB, i=2)[i],
                             tokb[:, 128 * i:128 * i + 128].rearrange("p (b w) -> p b w", b=NB)).then_inc(tok_out, 16)

        def program(eng, embed, layer, last, mlp):
            with eng.Fori(0, GROUPS) as g:
                embed(g)
                with eng.Fori(0, LAYERS - 1) as l:
                    layer(g, l)
                last(g)
                mlp(g)

        with nc.Block() as block:
            @block.tensor
            def _(pe):
                def embed(g):
                    for u in range(UNITS):
                        pe_embed(pe, g, u)
                        pe_main(pe, g, 0, u, None)
                        pe_forward(pe, g, 0, u, None)

                def layer(g, l):
                    for u in range(UNITS):
                        pe_inverse(pe, g, 1, u, l)
                        pe_main(pe, g, 1, u, l)
                        pe_forward(pe, g, 1, u, l)

                def last(g):
                    for u in range(UNITS):
                        pe_inverse(pe, g, LAYERS, u, None)
                        pe_main(pe, g, LAYERS, u, None)

                def mlp(g):
                    for u in range(UNITS):
                        pe_mlp(pe, g, u)

                program(pe, embed, layer, last, mlp)

            def drains(eng, j, main_of, mlp_of):
                def embed(g):
                    for u in range(UNITS):
                        drain_embed(eng, j, g, u)
                        main_of(eng, g, 0, u, None)
                        drain_forward(eng, j, g, 0, u, None)

                def layer(g, l):
                    for u in range(UNITS):
                        drain_inverse(eng, j, g, 1, u, l)
                        main_of(eng, g, 1, u, l)
                        drain_forward(eng, j, g, 1, u, l)

                def last(g):
                    for u in range(UNITS):
                        drain_inverse(eng, j, g, LAYERS, u, None)
                        main_of(eng, g, LAYERS, u, None)

                def mlp(g):
                    for u in range(UNITS):
                        mlp_of(eng, g, u)

                program(eng, embed, layer, last, mlp)

            @block.vector
            def _(dve):
                dve.memset(xs[:, :], 0.0).then_inc(xs_zero, 1)
                dve.wait_ge(xs_zero, 1)
                drains(dve, 0, dve_main, dve_mlp)

            @block.scalar
            def _(act):
                act.wait_ge(xs_zero, 1)
                drains(act, 1, act_main, act_mlp)

            @block.gpsimd
            def _(pool):
                def one(s):
                    def f(g, l=None):
                        for u in range(UNITS):
                            pool_main(pool, g, s, u, l)
                    return f
                program(pool, one(0), one(1), one(LAYERS), lambda g: None)

            @block.sync
            def _(sp):
                sp.dma_start(mixw[:, :], mix_scratch[0]).then_inc(mixw_in, 16)
                with sp.Fori(0, GROUPS) as g:
                    sp.wait_ge(main_full, g * CHUNKS_GROUP)
                    for u in range(UNITS):
                        sp_x(sp, g, u)
                    for u in range(UNITS):
                        sp_spectrum(sp, g, 0, u, None)
                    with sp.Fori(0, LAYERS - 1) as l:
                        for u in range(UNITS):
                            sp_bias(sp, g, 1, u, l)
                            if u == 0:
                                sp_mixw(sp, l + 1)
                            sp_spectrum(sp, g, 1, u, l)
                    for u in range(UNITS):
                        sp_bias(sp, g, LAYERS, u, None)
                        if u == 0:
                            sp_mixw(sp, 0)
                    for u in range(UNITS):
                        sp_tok(sp, g, u)
                sp.wait_ge(tok_out, GROUPS * UNITS * NB * 16)
                sp.wait_ge(mixw_in, (GROUPS * LAYERS + 1) * 16)


N_SMALL = 15 + NA * (1 + 2 + 2 * LAYERS + 1) + 4


TOK, D = IMGS * S, S
NT = TOK // 128
HEADS = 8
HP = HEADS // 2
QW = D * HEADS
HID, NE = 256, 8
NST = 256
ED = 128
DECAY, L1_EPS = 0.97, 1e-12
PADN = 96


def block_tables():
    f = np.float32
    s, q = np.meshgrid(np.arange(S), np.arange(S), indexing="ij")
    decay = np.where(s < q, DECAY ** np.maximum(q - 1 - s, 0), 0.0)
    return {
        "t_decay": np.concatenate([decay, decay]).astype(f),
        "t_diag": np.concatenate([np.eye(S)] * 2).astype(f),
        "t_rank": np.tile(np.arange(NE, 0, -1), (128, 1)).astype(f),
    }


def tables():
    return {**dft_tables(), **block_tables()}


def blocks(nc, t, tok, out, named):
    ctx = ExitStack()

    def sb(name, shape):
        return ctx.enter_context(nc.sbuf_tensor(name, shape, F32))

    def sems(tag, *names):
        return [named.enter_context(nc.semaphore(f"{tag}_{n}")) for n in names]

    with ctx:
        hid = sb("hid", [128, NT, D])
        z = sb("z", [128, NT, D])
        lv = sb("lv", [128, NT, D])
        zt = sb("zt", [128, TOK])
        big = sb("big", [128, 2, 4 * TOK])
        stat = sb("stat", [128, 6, NT])
        nhalf = sb("nhalf", [128, NT])
        ident = sb("ident2", [128, 128])
        wqkv = sb("wqkv", [128, 3 * QW])
        w0 = sb("w0", [128, HP, 2 * D])
        b0 = sb("b0", [128, D])
        w1 = sb("w1", [128, HID])
        wd = sb("wd", [128, 2, NE * D])
        wg = sb("wg", [128, 2, PADN])
        bd = sb("bd", [128, NE * D])
        bg = sb("bg", [128, NE])
        dxt = sb("dxt", [128, NST])
        dyt = sb("dyt", [128, NST])
        et = sb("et", [128, 2, PADN])
        decay = sb("decay", [128, S])
        diag = sb("diag", [128, S])
        rank = sb("rank", [128, NE])
        ones = sb("ones", [128, 128])
        gates = sb("gates", [128, 8, NT * NE])
        attn = gates[:, 0, :].rearrange("p (i e) -> p i e", e=NE)
        x1 = sb("x1w", [128, NE * ED])
        x2 = sb("x2w", [128, NE, D])
        xg = sb("xg", [128, PADN])
        x2b = sb("x2b", [128, NE * D])
        ps = [ctx.enter_context(nc.psum_tensor(f"bank{i}", [128, 512], F32)) for i in range(8)]
        raww = big[0:64, 1, 0:3 * QW]
        rawd = big[:, 1, 2048:2048 + 4 * D].rearrange("p (k n) -> p k n", n=D)
        rawe = big[0:64, 1, 2560:2560 + NST]

        w_zero, w_in, w_pe, w_rdy = sems("w", "zero", "in", "pe", "rdy")
        loads = [(ident[:, :], t["t_ident"]), (decay[:, :], t["t_decay"]), (diag[:, :], t["t_diag"]),
                 (rank[:, :], t["t_rank"]), (raww, t["L0_attn_Wqkv"]),
                 (big[64:65, 1, 0:3 * QW], t["L0_attn_bqkv"].rearrange("(a n) -> a n", a=1)),
                 (b0[:, :], t["L0_attn_b0"].rearrange("(a n) -> a n", a=1).to_broadcast([128, D])),
                 (w1[0:D, :], t["L0_ffn_W1"]), (w1[D:D + 1, :], t["L0_ffn_b1"].rearrange("(a n) -> a n", a=1)),
                 (bd[:, :], t["L0_ffn_bd"].rearrange("(a e) n -> a (e n)", a=1).to_broadcast([128, NE * D])),
                 (bg[:, :], t["L0_ffn_bg"].rearrange("(a n) -> a n", a=1).to_broadcast([128, NE])),
                 (rawe, t["L1_attn_E"]),
                 (rawd[:, 0:2, :], t["L1_attn_Dx"].rearrange("(k p) d -> p k d", p=128)),
                 (rawd[:, 2:4, :], t["L1_attn_Dy"].rearrange("(k p) d -> p k d", p=128)),
                 (x1[0:D, :].rearrange("p (e n) -> p e n", e=NE), t["L1_ffn_W1"].rearrange("e d n -> d e n")),
                 (x1[D:D + 1, :], t["L1_ffn_b1"].rearrange("(a e) n -> a (e n)", a=1)),
                 (x2[:, :, :], t["L1_ffn_W2"].rearrange("e p n -> p e n")),
                 (x2b[:, :], t["L1_ffn_b2"].rearrange("(a e) n -> a (e n)", a=1).to_broadcast([128, NE * D])),
                 (xg[0:D, 0:NE], t["L1_ffn_Wg"]), (xg[D:D + 1, 0:NE], t["L1_ffn_bg"].rearrange("(a n) -> a n", a=1)),
                 (xg[D + 1:D + 2, 0:NE], t["L1_ffn_bias"].rearrange("(a n) -> a n", a=1)),
                 (hid[:, :, :], tok.rearrange("(i b) r w -> (b r) i w", b=2))]
        for k in range(2):
            loads.append((wd[:, k, :].rearrange("p (e n) -> p e n", e=NE),
                          t["L0_ffn_Wd"].rearrange("e (k p) n -> k p e n", k=2)[k]))
            loads.append((wg[:, k, 0:NE], t["L0_ffn_Wg"].rearrange("(k p) n -> k p n", k=2)[k]))
            for hp in range(HP):
                loads.append((w0[64 * k:64 * k + 64, hp, D * k:D * k + D],
                              t["L0_attn_W0"].rearrange("(d h) n -> h d n", h=HEADS)[2 * hp + k]))
        with nc.Block() as block:
            @block.vector
            def _(dve):
                zeros = [wqkv[:, :], w0[:, :, :], w1[:, :], wg[:, :, :], dxt[:, :], dyt[:, :], et[:, :, :],
                         x1[:, :], xg[:, :]]
                for v in zeros:
                    dve.memset(v, 0.0).then_inc(w_zero, 1)
                dve.memset(zt[64:128, :], 1.0).then_inc(w_zero, 1)
                dve.memset(nhalf[:, :], -0.5).then_inc(w_zero, 1)
                dve.memset(ones[:, :], 1.0).then_inc(w_zero, 1)
                dve.wait_ge(w_zero, 12)
                dve.wait_ge(w_in, 16 * len(loads))
                dve.tensor_copy(wqkv[0:65, :].rearrange("p (s h d) -> p s h d", s=3, h=HEADS),
                                big[0:65, 1, 0:3 * QW].rearrange("p (s d h) -> p s h d", s=3, h=HEADS))
                dve.wait_ge(w_pe, 1)
                for k in range(2):
                    dve.tensor_copy(dxt[0:64, 128 * k:128 * k + 128], ps[0][0:64, 128 * k:128 * k + 128])
                    dve.tensor_copy(dyt[0:64, 128 * k:128 * k + 128], ps[0][0:64, 256 + 128 * k:256 + 128 * k + 128])
                    dve.tensor_copy(et[:, k, 0:D], ps[1][:, 64 * k:64 * k + 64])

            @block.sync
            def _(sp):
                sp.wait_ge(w_zero, 12)
                for dst, src in loads:
                    sp.dma_start(dst, src).then_inc(w_in, 16)

            @block.tensor
            def _(pe):
                pe.wait_ge(w_in, 16 * len(loads))
                for k in range(4):
                    pe.transpose(ps[0][0:64, 128 * k:128 * k + 128], rawd[:, k, :], ident[:, :])
                for k in range(2):
                    mm = pe.transpose(ps[1][:, 64 * k:64 * k + 64], rawe[:, 128 * k:128 * k + 128], ident[0:64, 0:64])
                mm.then_inc(w_pe, 1)

        s_sum, s_cen, s_sq, s_red, s_var, s_rstd, s_out, s_t, s_ev, s_add = sems(
            "norm", "sum", "cen", "sq", "red", "var", "rstd", "out", "t", "ev", "add")
        PARTS = 4

        def normalise(call, src, dst, residual=None, transpose=None):
            n, parts = NT // PARTS, PARTS
            p0 = call * PARTS
            t0 = (transpose or 0) * (NT // 4)
            cen = big[:, 0, 0:NT * D].rearrange("p (i d) -> p i d", d=D)
            sqr = big[:, 0, NT * D:2 * NT * D].rearrange("p (i d) -> p i d", d=D)
            with nc.Block() as block:
                @block.vector
                def _(dve):
                    for k in range(parts + 2):
                        if k < parts:
                            i = slice(n * k, n * k + n)
                            dve.tensor_reduce(stat[:, 0, i], src[:, i, :], AX.X, ALU.add).then_inc(s_sum, 1)
                            dve.wait_ge(s_sum, p0 + k + 1)
                            dve.scalar_tensor_tensor(out=cen[:, i, :], in0=stat[:, 0, i].unsqueeze(2).to_broadcast([128, n, D]),
                                                     scalar=-1.0 / D, in1=src[:, i, :], op0=ALU.mult,
                                                     op1=ALU.add).then_inc(s_cen, 1)
                        if 1 <= k <= parts:
                            i = slice(n * (k - 1), n * k)
                            dve.wait_ge(s_sq, p0 + k)
                            dve.tensor_reduce(stat[:, 1, i], sqr[:, i, :], AX.X, ALU.add).then_inc(s_red, 1)
                        if k >= 2:
                            i = slice(n * (k - 2), n * (k - 1))
                            dve.wait_ge(s_rstd, p0 + k - 1)
                            dve.tensor_tensor(dst[:, i, :], cen[:, i, :],
                                              stat[:, 3, i].unsqueeze(2).to_broadcast([128, n, D]),
                                              ALU.mult).then_inc(s_out, 1)
                            if residual is not None:
                                dve.wait_ge(s_out, p0 + k - 1)
                                dve.tensor_tensor(residual[:, i, :], residual[:, i, :], dst[:, i, :], ALU.add).then_inc(s_add, 1)
                    if transpose is not None:
                        for k in range(0, NT // 4, 2):
                            dve.wait_ge(s_t, t0 + k + 1)
                            dve.tensor_copy(zt[0:64, 512 * k:512 * k + 512], ps[k][0:64, :]).then_inc(s_ev, 1)

                @block.scalar
                def _(act):
                    for k in range(parts):
                        i = slice(n * k, n * k + n)
                        act.wait_ge(s_cen, p0 + k + 1)
                        act.activation(sqr[:, i, :], cen[:, i, :], ACT.Square).then_inc(s_sq, 1)
                    if transpose is not None:
                        for k in range(1, NT // 4, 2):
                            act.wait_ge(s_t, t0 + k + 1)
                            act.copy(zt[0:64, 512 * k:512 * k + 512], ps[k][0:64, :]).then_inc(s_ev, 1)

                @block.gpsimd
                def _(pool):
                    for k in range(parts):
                        i = slice(n * k, n * k + n)
                        pool.wait_ge(s_red, p0 + k + 1)
                        pool.tensor_scalar(stat[:, 2, i], stat[:, 1, i], 1.0 / D, EPS, ALU.mult, ALU.add).then_inc(s_var, 1)
                        pool.wait_ge(s_var, p0 + k + 1)
                        pool.tensor_tensor(stat[:, 3, i], stat[:, 2, i], nhalf[:, i], ALU.pow).then_inc(s_rstd, 1)

                if transpose is not None:
                    @block.tensor
                    def _(pe):
                        for k in range(NT // 4):
                            pe.wait_ge(s_out, p0 + k // 2 + 1)
                            for i in range(4):
                                mm = pe.transpose(ps[k][0:64, 128 * i:128 * i + 128], dst[:, 4 * k + i, :], ident[:, :])
                            mm.then_inc(s_t, 1)

        normalise(0, hid, z, transpose=0)

        def project(pe, bank, section, hp, r0):
            first = section * TOK + r0
            for seg in range(3):
                m0 = -(-(first - seg) // 3)
                m1 = (first + 511 - seg) // 3 + 1
                at = 3 * m0 + seg - first
                w = (seg * HEADS + 2 * hp) * D
                mm = pe.matmul(bank[:, at:at + 3 * (m1 - m0 - 1) + 1:3], wqkv[:, w:w + 128], zt[:, m0:m1],
                               start=True, stop=True, skip_group_check=True)
            return mm

        a_full, a_e0, a_e1 = sems("qk", "full", "free0", "free1")
        jobs = [(sec, hp, r) for r in range(0, TOK, 512) for sec in range(2) for hp in range(HP)]
        qk = big[:, :, :].rearrange("p s (h r) -> p s h r", h=HP)
        with nc.Block() as block:
            @block.tensor
            def _(pe):
                for n, (sec, hp, r) in enumerate(jobs):
                    if n >= 8:
                        pe.wait_ge((a_e0, a_e1)[n % 2], n // 2 - 3)
                    project(pe, ps[n % 8], sec, hp, r).then_inc(a_full, 1)

            @block.vector
            def _(dve):
                for n in range(0, len(jobs), 2):
                    sec, hp, r = jobs[n]
                    dve.wait_ge(a_full, n + 1)
                    dve.tensor_copy(qk[:, sec, hp, r:r + 512], ps[n % 8][:, :]).then_inc(a_e0, 1)

            @block.scalar
            def _(act):
                for n in range(1, len(jobs), 2):
                    sec, hp, r = jobs[n]
                    act.wait_ge(a_full, n + 1)
                    act.copy(qk[:, sec, hp, r:r + 512], ps[n % 8][:, :]).then_inc(a_e1, 1)

        c_full, c_max, c_sub, c_exp, c_sum, c_msk, c_dg, c_rc, c_at = sems(
            "sc", "full", "max", "sub", "exp", "sum", "msk", "dg", "rc", "at")
        NS_ = NT // 2 * 2
        sub = gates[:, 2:4, :].rearrange("p a n -> p (a n)").rearrange("p (b n) -> p b n", b=1)
        shifted = lv[:, :, :].rearrange("p (b i) d -> p b (i d)", b=4)
        masked = z[:, :, :].rearrange("p (b i) d -> p b (i d)", b=4)
        G8 = [128, 8, S]
        with nc.Block() as block:
            @block.tensor
            def _(pe):
                for n in range(NS_):
                    j, par = n // 2, n % 2
                    if n >= 8:
                        pe.wait_ge(c_sub, n - 7)
                    rows = slice(64 * par, 64 * par + 64)
                    for i in range(2):
                        for b in range(2):
                            r = ((2 * j + i) * 2 + b) * S
                            for hp in range(HP):
                                col = (i * HP + hp) * S
                                mm = pe.matmul(ps[n % 8][64 * b:64 * b + 64, col:col + S], qk[rows, 1, hp, r:r + S],
                                               qk[rows, 0, hp, r:r + S], start=True, stop=True)
                    mm.then_inc(c_full, 1)

            @block.vector
            def _(dve):
                lag = 2
                for n in range(NS_ + lag):
                    if n < NS_:
                        dve.wait_ge(c_full, n + 1)
                        b = ps[n % 8][:, :].rearrange("p (g s) -> p g s", s=S)
                        mx = gates[:, 1, 8 * (n % 4):8 * (n % 4) + 8]
                        dve.tensor_reduce(mx, b, AX.X, ALU.max).then_inc(c_max, 1)
                        dve.wait_ge(c_max, n + 1)
                        if n >= 4:
                            dve.wait_ge(c_msk, n - 3)
                        dve.tensor_tensor(shifted[:, n % 4, :].rearrange("p (g s) -> p g s", s=S), b,
                                          mx.unsqueeze(2).to_broadcast(G8), ALU.subtract).then_inc(c_sub, 1)
                    if n >= lag:
                        d = n - lag
                        j, par = d // 2, d % 2
                        e = shifted[:, d % 4, :].rearrange("p (g s) -> p g s", s=S)
                        m = masked[:, d % 4, :].rearrange("p (g s) -> p g s", s=S)
                        dve.wait_ge(c_exp, d + 1)
                        dve.tensor_reduce(gates[:, 2, 8 * d:8 * d + 8], e, AX.X, ALU.add).then_inc(c_sum, 1)
                        if d >= 4:
                            dve.wait_ge(c_dg, d - 3)
                        dve.tensor_tensor(m, e, diag[:, :].unsqueeze(1).to_broadcast(G8), ALU.mult).then_inc(c_msk, 1)
                        dve.wait_ge(c_msk, d + 1)
                        dve.tensor_reduce(gates[:, 3, 8 * d:8 * d + 8], m, AX.X, ALU.add).then_inc(c_dg, 1)
                dve.wait_ge(c_sum, NS_)
                dve.reciprocal(gates[:, 4, :], gates[:, 2, :]).then_inc(c_rc, 1)
                dve.wait_ge(c_rc, 1)
                dve.wait_ge(c_dg, NS_)
                for par in range(2):
                    for i in range(2):
                        def v(k):
                            return gates[:, k, :].rearrange("p (j q i h) -> p q i j h", q=2, i=2, h=HP)[:, par, i]
                        o = gates[:, 0, :].rearrange("p (j i h q) -> p q i j h", i=2, q=2, h=HP)[:, par, i]
                        dve.tensor_tensor(o, v(3), v(4), ALU.mult).then_inc(c_at, 1)

            @block.scalar
            def _(act):
                for n in range(NS_):
                    act.wait_ge(c_sub, n + 1)
                    act.activation(shifted[:, n % 4, :], shifted[:, n % 4, :], ACT.Exp, scale=float(D) ** -0.5).then_inc(c_exp, 1)

        v_full, v_sb, v_p, v_w, v_r, v_a = sems("v", "full", "sb", "p", "w", "r", "a")
        NCK = TOK // 512
        vt = big[:, 0, 0:2 * HP * 512].rearrange("p (b h r) -> p b h r", b=2, h=HP)
        wtd = big[:, 1, 0:2 * 512].rearrange("p (b n) -> p b n", b=2)
        red = big[:, 1, 2048:2048 + 2 * D].rearrange("p (b n) -> p b n", b=2)
        with nc.Block() as block:
            @block.tensor
            def _(pe):
                for c in range(NCK + 1):
                    if c < NCK:
                        for hp in range(HP):
                            if c >= 1:
                                pe.wait_ge(v_sb, HP * (c - 1) + hp + 1)
                            project(pe, ps[hp], 2, hp, 512 * c).then_inc(v_full, 1)
                    if c >= 1:
                        for i in range(4):
                            n = 4 * (c - 1) + i
                            pe.wait_ge(v_sb, HP * c)
                            if n >= 4:
                                pe.wait_ge(v_w, n - 3)
                            for hp in range(HP):
                                mm = pe.matmul(ps[4 + n % 4][:, 128 * hp:128 * hp + 128],
                                               vt[:, (c - 1) % 2, hp, 128 * i:128 * i + 128], w0[:, hp, :], start=True, stop=True)
                            mm.then_inc(v_p, 1)

            @block.scalar
            def _(act):
                for c in range(NCK):
                    for hp in range(HP):
                        act.wait_ge(v_full, HP * c + hp + 1)
                        if c >= 2:
                            act.wait_ge(v_p, 4 * (c - 1))
                        act.copy(vt[:, c % 2, hp, :], ps[hp][:, :]).then_inc(v_sb, 1)

            @block.vector
            def _(dve):
                for n in range(NT):
                    dve.wait_ge(v_p, n + 1)
                    if n >= 2:
                        dve.wait_ge(v_r, n - 1)
                    w = wtd[:, n % 2, :]
                    dve.tensor_tensor(w.rearrange("p (h d) -> p h d", d=D), ps[4 + n % 4][:, :].rearrange("p (h d) -> p h d", d=D),
                                      attn[:, n, :].unsqueeze(2).to_broadcast([128, HEADS, D]), ALU.mult).then_inc(v_w, 1)
                    dve.wait_ge(v_w, n + 1)
                    if n >= 2:
                        dve.wait_ge(v_a, 2 * (n - 1))
                    dve.tensor_reduce(red[:, n % 2, :], w.rearrange("p (h d) -> p d h", d=D), AX.X, ALU.add).then_inc(v_r, 1)
                    dve.wait_ge(v_r, n + 1)
                    dve.tensor_tensor(hid[:, n, :], hid[:, n, :], red[:, n % 2, :], ALU.add).then_inc(v_a, 1)
                    dve.wait_ge(v_a, 2 * n + 1)
                    dve.tensor_tensor(hid[:, n, :], hid[:, n, :], b0[:, :], ALU.add).then_inc(v_a, 1)

        def first_max(dve, sem_, count, logits, top, pick):
            v3 = lambda a: a.rearrange("p (i e) -> p i e", e=NE)
            b = lambda a: a.unsqueeze(2).to_broadcast([128, NT, NE])
            steps = [lambda: dve.tensor_reduce(top, v3(logits), AX.X, ALU.max),
                     lambda: dve.tensor_tensor(v3(pick), v3(logits), b(top), ALU.is_equal),
                     lambda: dve.tensor_tensor(v3(pick), v3(pick), rank[:, :].unsqueeze(1).to_broadcast([128, NT, NE]), ALU.mult),
                     lambda: dve.tensor_reduce(stat[:, 5, :], v3(pick), AX.X, ALU.max),
                     lambda: dve.tensor_tensor(v3(pick), v3(pick), b(stat[:, 5, :]), ALU.is_equal)]
            for step in steps:
                step().then_inc(sem_, 1)
                count += 1
                dve.wait_ge(sem_, count)
            return count

        def combine(dve, bank, n, bias, weights, s_b, s_w, s_r, s_a):
            acc = big[:, 1, 12288 + 1024 * (n % 2):12288 + 1024 * (n % 2) + 512]
            wt = big[:, 1, 12800 + 1024 * (n % 2):12800 + 1024 * (n % 2) + 512]
            if n >= 2:
                dve.wait_ge(s_w, n - 1)
            dve.tensor_tensor(acc, bank, bias, ALU.add).then_inc(s_b, 1)
            dve.wait_ge(s_b, n + 1)
            if n >= 2:
                dve.wait_ge(s_r, n - 1)
            dve.tensor_tensor(wt.rearrange("p (e d) -> p e d", d=D), acc.rearrange("p (e d) -> p e d", d=D),
                              weights[:, NE * n:NE * n + NE].unsqueeze(2).to_broadcast([128, NE, D]), ALU.mult).then_inc(s_w, 1)
            dve.wait_ge(s_w, n + 1)
            if n >= 2:
                dve.wait_ge(s_a, n - 1)
            r = big[:, 1, 14336 + 64 * (n % 2):14336 + 64 * (n % 2) + 64]
            dve.tensor_reduce(r, wt.rearrange("p (e d) -> p d e", d=D), AX.X, ALU.add).then_inc(s_r, 1)
            dve.wait_ge(s_r, n + 1)
            dve.tensor_tensor(hid[:, n, :], hid[:, n, :], r, ALU.add).then_inc(s_a, 1)

        normalise(1, hid, z, transpose=1)
        f_full, f_h, f_g, f_lg, f_gt, f_exp, f_y, f_b, f_w, f_r, f_a = sems(
            "f", "full", "h", "g", "lg", "gt", "exp", "y", "b", "w", "r", "a")
        ht = big[:, 0, 0:2 * TOK].rearrange("p (k n) -> p k n", k=2)
        logits, top, pick, ex = gates[:, 1, :], stat[:, 4, :], gates[:, 2, :], gates[:, 3, :]
        with nc.Block() as block:
            @block.tensor
            def _(pe):
                for n in range(16):
                    if n >= 4:
                        pe.wait_ge(f_h, n - 3)
                    k, c = n % 2, n // 2
                    pe.matmul(ps[n % 4][:, :], w1[:, 128 * k:128 * k + 128], zt[:, 512 * c:512 * c + 512],
                              start=True, stop=True).then_inc(f_full, 1)
                pe.wait_ge(f_h, 16)
                for n in range(NT):
                    b, o = 4 + n // 4 % 2, 100 * (n % 4)
                    if n % 4 == 0 and n >= 8:
                        pe.wait_ge(f_lg, n // 4 - 1)
                    for k in range(2):
                        mm = pe.matmul(ps[b][:, o:o + PADN], ht[:, k, 128 * n:128 * n + 128], wg[:, k, :],
                                       start=(k == 0), stop=(k == 1))
                    if n % 4 == 3:
                        mm.then_inc(f_g, 1)
                for n in range(NT):
                    if n >= 4:
                        pe.wait_ge(f_b, n - 3)
                    for k in range(2):
                        mm = pe.matmul(ps[n % 4][:, :], ht[:, k, 128 * n:128 * n + 128], wd[:, k, :],
                                       start=(k == 0), stop=(k == 1))
                    mm.then_inc(f_y, 1)

            @block.scalar
            def _(act):
                for n in range(16):
                    act.wait_ge(f_full, n + 1)
                    act.activation(ht[:, n % 2, 512 * (n // 2):512 * (n // 2) + 512], ps[n % 4][:, :], ACT.Gelu).then_inc(f_h, 1)
                act.wait_ge(f_gt, 6)
                act.activation(ex, ex, ACT.Exp).then_inc(f_exp, 1)

            @block.vector
            def _(dve):
                v3 = lambda a: a.rearrange("p (i e) -> p i e", e=NE)
                for n in range(NT // 4):
                    dve.wait_ge(f_g, n + 1)
                    dve.tensor_tensor(v3(logits)[:, 4 * n:4 * n + 4, :],
                                      ps[4 + n % 2][:, 0:400].rearrange("p (i e) -> p i e", i=4)[:, :, 0:NE],
                                      bg[:, :].unsqueeze(1).to_broadcast([128, 4, NE]), ALU.add).then_inc(f_lg, 1)
                dve.wait_ge(f_lg, NT // 4)
                count = first_max(dve, f_gt, 0, logits, top, pick)
                b = lambda a: a.unsqueeze(2).to_broadcast([128, NT, NE])
                dve.tensor_tensor(v3(ex), v3(logits), b(top), ALU.subtract).then_inc(f_gt, 1)
                dve.wait_ge(f_exp, 1)
                dve.tensor_reduce(stat[:, 0, :], v3(ex), AX.X, ALU.add).then_inc(f_gt, 1)
                dve.wait_ge(f_gt, count + 2)
                dve.reciprocal(stat[:, 1, :], stat[:, 0, :]).then_inc(f_gt, 1)
                dve.wait_ge(f_gt, count + 3)
                dve.tensor_tensor(v3(pick), v3(pick), b(stat[:, 1, :]), ALU.mult).then_inc(f_gt, 1)
                dve.wait_ge(f_gt, count + 4)
                for n in range(NT):
                    dve.wait_ge(f_y, n + 1)
                    combine(dve, ps[n % 4][:, :], n, bd[:, :], pick, f_b, f_w, f_r, f_a)

        normalise(2, hid, z, transpose=2)
        normalise(3, z, lv)
        r_full, r_x, r_rf, r_rs, r_s, r_d, r_b, r_sc = sems("r", "full", "x", "rf", "rs", "s", "d", "b", "sc")
        rt = big[:, 0, 0:2 * TOK].rearrange("p (k n) -> p k n", k=2)
        rb = big[:, 0, 2 * TOK:3 * TOK]
        ss = big[:, 0, 3 * TOK:4 * TOK]
        av = big[:, 1, 0:TOK]
        rec = big[:, 1, TOK:2 * TOK]
        xt = big[:, 1, 2 * TOK:4 * TOK].rearrange("p (k n) -> p k n", k=2)
        carry = ones[:, 64:128]
        cbuf = stat[:, 0:2, :].rearrange("p a n -> p (a n)")
        with nc.Block() as block:
            @block.tensor
            def _(pe):
                for n in range(16):
                    if n >= 4:
                        pe.wait_ge(r_x, n - 3)
                    k, c = n % 2, n // 2
                    pe.matmul(ps[n % 4][:, :], dxt[:, 128 * k:128 * k + 128], zt[:, 512 * c:512 * c + 512],
                              start=True, stop=True).then_inc(r_full, 1)
                for c in range(8):
                    pe.wait_ge(r_x, 2 * c + 2)
                    if c >= 4:
                        pe.wait_ge(r_rs, c - 3)
                    for k in range(2):
                        mm = pe.matmul(ps[4 + c % 4][:, :], ones[:, :], rt[:, k, 512 * c:512 * c + 512],
                                       start=(k == 0), stop=(k == 1))
                    mm.then_inc(r_rf, 1)

            @block.scalar
            def _(act):
                for n in range(16):
                    act.wait_ge(r_full, n + 1)
                    act.activation(rt[:, n % 2, 512 * (n // 2):512 * (n // 2) + 512], ps[n % 4][:, :], ACT.Relu).then_inc(r_x, 1)
                for c in range(8):
                    act.wait_ge(r_rf, c + 1)
                    act.copy(rb[:, 512 * c:512 * c + 512], ps[4 + c % 4][:, :]).then_inc(r_rs, 1)

            @block.vector
            def _(dve):
                sv = ss.rearrange("p (b t) -> p t b", t=S)
                rv = rb.rearrange("p (b t) -> p t b", t=S)
                dve.wait_ge(r_rs, 8)
                dve.tensor_copy(sv[:, 0, :], rv[:, 0, :]).then_inc(r_s, 1)
                for i in range(1, S):
                    dve.wait_ge(r_s, 2 * i - 1)
                    dve.tensor_scalar(cbuf, sv[:, i - 1, :], DECAY / L1_EPS, DECAY, ALU.mult, ALU.min).then_inc(r_s, 1)
                    dve.wait_ge(r_s, 2 * i)
                    dve.tensor_tensor(sv[:, i, :], cbuf, rv[:, i, :], ALU.add).then_inc(r_s, 1)
                dve.wait_ge(r_s, 2 * S - 1)
                dve.tensor_scalar(ss, ss, L1_EPS, None, ALU.max).then_inc(r_d, 1)
                dve.wait_ge(r_d, 1)
                dve.reciprocal(rec, ss).then_inc(r_d, 1)
                dve.wait_ge(r_d, 2)
                dve.tensor_scalar(av, rec, DECAY, None, ALU.mult).then_inc(r_d, 1)
                dve.wait_ge(r_d, 3)
                dve.memset(av.rearrange("p (b t) -> p t b", t=S)[:, 0, :], 0.0).then_inc(r_d, 1)
                for k in range(2):
                    dve.tensor_tensor(rt[:, k, :], rt[:, k, :], rec, ALU.mult).then_inc(r_b, 1)
                dve.wait_ge(r_d, 4)
                dve.wait_ge(r_b, 2)
                for k in range(2):
                    dve.tensor_tensor_scan(xt[:, k, :], av, rt[:, k, :], 0.0, ALU.mult, ALU.add).then_inc(r_sc, 1)

        g_full, g_m, g_a, g_ev = sems("g", "full", "m", "a", "ev")
        gm = big[:, 0, 0:NT * S].rearrange("p (i t) -> p i t", t=S)
        with nc.Block() as block:
            @block.tensor
            def _(pe):
                for c in range(NT // 8):
                    for i in range(8):
                        for b in range(2):
                            n = ((8 * c + i) * 2 + b) * S
                            for k in range(2):
                                mm = pe.matmul(ps[c][64 * b:64 * b + 64, S * i:S * i + S], xt[:, k, n:n + S], xt[:, k, n:n + S],
                                               start=(k == 0), stop=(k == 1))
                    mm.then_inc(g_full, 1)
                for b in range(2):
                    for c in range(NT // 8):
                        if b:
                            pe.wait_ge(g_ev, c + 1)
                        pe.wait_ge(g_m, c + 1)
                        rows = slice(64 * b, 64 * b + 64)
                        for i in range(8):
                            n = 8 * c + i
                            mm = pe.matmul(ps[4 + c][rows, D * i:D * i + D], gm[rows, n, :], lv[rows, n, :], start=True, stop=True)
                        mm.then_inc(g_a, 1)

            @block.vector
            def _(dve):
                for c in range(NT // 8):
                    dve.wait_ge(g_full, c + 1)
                    dve.tensor_tensor(gm[:, 8 * c:8 * c + 8, :], ps[c][:, :].rearrange("p (i t) -> p i t", t=S),
                                      decay[:, :].unsqueeze(1).to_broadcast([128, 8, S]), ALU.mult).then_inc(g_m, 1)
                for b in range(2):
                    for c in range(NT // 8):
                        dve.wait_ge(g_a, (NT // 8) * b + c + 1)
                        rows = slice(64 * b, 64 * b + 64)
                        dve.tensor_copy(z[rows, 8 * c:8 * c + 8, :], ps[4 + c][rows, :].rearrange("p (i d) -> p i d", d=D)).then_inc(g_ev, 1)

        normalise(4, z, lv, transpose=3)
        y_full, y_y, y_v, y_ev = sems("y", "full", "y", "v", "ev")
        yt = big[:, 0, 0:2 * TOK].rearrange("p (k n) -> p k n", k=2)
        with nc.Block() as block:
            @block.tensor
            def _(pe):
                for n in range(16):
                    if n >= 4:
                        pe.wait_ge(y_y, n - 3)
                    k, c = n % 2, n // 2
                    pe.matmul(ps[n % 4][:, :], dyt[:, 128 * k:128 * k + 128], zt[:, 512 * c:512 * c + 512],
                              start=True, stop=True).then_inc(y_full, 1)
                for n in range(NT):
                    pe.wait_ge(y_y, 2 * (n // 4) + 2)
                    if n % 4 == 0 and n >= 16:
                        pe.wait_ge(y_ev, n // 4 - 3)
                    o = ps[4 + n // 4 % 4][:, 100 * (n % 4):100 * (n % 4) + PADN]
                    for k in range(2):
                        mm = pe.matmul(o, yt[:, k, 128 * n:128 * n + 128], et[:, k, :], start=(k == 0), stop=(k == 1))
                    if n % 4 == 3:
                        mm.then_inc(y_v, 1)

            @block.vector
            def _(dve):
                for n in range(16):
                    dve.wait_ge(y_full, n + 1)
                    k, c = n % 2, slice(512 * (n // 2), 512 * (n // 2) + 512)
                    dve.scalar_tensor_tensor(out=yt[:, k, c], in0=ps[n % 4][:, :], scalar=0.0, in1=xt[:, k, c],
                                             op0=ALU.max, op1=ALU.mult).then_inc(y_y, 1)

            @block.scalar
            def _(act):
                for n in range(NT // 4):
                    act.wait_ge(y_v, n + 1)
                    act.copy(z[:, 4 * n:4 * n + 4, :],
                             ps[4 + n % 4][:, 0:400].rearrange("p (i d) -> p i d", i=4)[:, :, 0:D]).then_inc(y_ev, 1)

        normalise(5, z, lv, residual=hid)
        normalise(6, hid, z, transpose=4)
        e_g, e_lg, e_gt, e_exp, e_full, e_h, e_y, e_b, e_w, e_r, e_a, e_out = sems(
            "e", "g", "lg", "gt", "exp", "full", "h", "y", "b", "w", "r", "a", "out")
        logits2, pick2, cmb = gates[:, 4, :], gates[:, 5, :], gates[:, 6, :]
        eh = big[:, 0, 0:2 * NE * 512].rearrange("p (b e n) -> p b e n", b=2, e=NE)
        with nc.Block() as block:
            @block.tensor
            def _(pe):
                for n in range(NT):
                    b, o = 4 + n // 4 % 4, 100 * (n % 4)
                    if n % 4 == 0 and n >= 16:
                        pe.wait_ge(e_lg, n // 4 - 3)
                    mm = pe.matmul(ps[b][:, o:o + PADN], zt[:, 128 * n:128 * n + 128], xg[:, :], start=True, stop=True)
                    if n % 4 == 3:
                        mm.then_inc(e_g, 1)
                pe.wait_ge(e_lg, NT // 4)
                for c in range(NCK + 1):
                    if c < NCK:
                        for e in range(NE):
                            n = NE * c + e
                            if n >= 4:
                                pe.wait_ge(e_h, n - 3)
                            pe.matmul(ps[n % 4][:, :], x1[:, ED * e:ED * e + ED], zt[:, 512 * c:512 * c + 512],
                                      start=True, stop=True).then_inc(e_full, 1)
                    if c >= 1:
                        for i in range(4):
                            n = 4 * (c - 1) + i
                            pe.wait_ge(e_h, NE * c)
                            if n >= 4:
                                pe.wait_ge(e_b, n - 3)
                            for e in range(NE):
                                w = PADN if e < NE - 1 else D
                                mm = pe.matmul(ps[4 + n % 4][:, D * e:D * e + w], eh[:, (c - 1) % 2, e, 128 * i:128 * i + 128],
                                               x2[:, :, :].rearrange("p e d -> p (e d)")[:, D * e:D * e + w],
                                               start=True, stop=True, skip_group_check=True)
                            mm.then_inc(e_y, 1)

            @block.scalar
            def _(act):
                act.wait_ge(e_gt, 14)
                act.activation(stat[:, 3, :], stat[:, 2, :], ACT.Exp).then_inc(e_exp, 1)
                for n in range(NE * NCK):
                    c, e = n // NE, n % NE
                    act.wait_ge(e_full, n + 1)
                    if c >= 2:
                        act.wait_ge(e_y, 4 * (c - 1))
                    act.activation(eh[:, c % 2, e, :], ps[n % 4][:, :], ACT.Relu).then_inc(e_h, 1)

            @block.vector
            def _(dve):
                v3 = lambda a: a.rearrange("p (i e) -> p i e", e=NE)
                b = lambda a: a.unsqueeze(2).to_broadcast([128, NT, NE])
                for n in range(NT // 4):
                    dve.wait_ge(e_g, n + 1)
                    dve.tensor_copy(v3(logits)[:, 4 * n:4 * n + 4, :],
                                    ps[4 + n % 4][:, 0:400].rearrange("p (i e) -> p i e", i=4)[:, :, 0:NE]).then_inc(e_lg, 1)
                dve.wait_ge(e_lg, NT // 4)
                count = first_max(dve, e_gt, 0, logits, stat[:, 0, :], pick)
                dve.tensor_scalar(pick2, pick, -1e30, None, ALU.mult).then_inc(e_gt, 1)
                dve.wait_ge(e_gt, count + 1)
                dve.tensor_tensor(logits2, logits, pick2, ALU.add).then_inc(e_gt, 1)
                count += 2
                dve.wait_ge(e_gt, count)
                count = first_max(dve, e_gt, count, logits2, stat[:, 1, :], pick2)
                dve.tensor_tensor(stat[:, 2, :], stat[:, 1, :], stat[:, 0, :], ALU.subtract).then_inc(e_gt, 1)
                dve.wait_ge(e_gt, count + 1)
                dve.tensor_copy(stat[:, 4, :], stat[:, 2, :]).then_inc(e_gt, 1)
                count += 2
                dve.wait_ge(e_exp, 1)
                steps = [lambda: dve.tensor_scalar(stat[:, 4, :], stat[:, 3, :], 1.0, None, ALU.add),
                         lambda: dve.reciprocal(stat[:, 5, :], stat[:, 4, :]),
                         lambda: dve.tensor_tensor(stat[:, 4, :], stat[:, 5, :], stat[:, 3, :], ALU.mult),
                         lambda: dve.tensor_tensor(v3(pick), v3(pick), b(stat[:, 5, :]), ALU.mult),
                         lambda: dve.tensor_tensor(v3(pick2), v3(pick2), b(stat[:, 4, :]), ALU.mult),
                         lambda: dve.tensor_tensor(cmb, pick, pick2, ALU.add)]
                dve.wait_ge(e_gt, count)
                for step in steps:
                    step().then_inc(e_gt, 1)
                    count += 1
                    dve.wait_ge(e_gt, count)
                for n in range(NT):
                    dve.wait_ge(e_y, n + 1)
                    combine(dve, ps[4 + n % 4][:, :], n, x2b[:, :], cmb, e_b, e_w, e_r, e_a)

            @block.sync
            def _(sp):
                for c in range(NT // 8):
                    sp.wait_ge(e_a, 8 * c + 8)
                    sp.dma_start(out.rearrange("(i b) r w -> (b r) i w", b=2)[:, 8 * c:8 * c + 8, :],
                                 hid[:, 8 * c:8 * c + 8, :]).then_inc(e_out, 16)
                sp.wait_ge(e_out, 16 * (NT // 8))


def build(nc, t, out):
    tok = nc.dram_tensor("tok", (IMGS, S, S), F32, kind="Internal").ap()
    with ExitStack() as named:
        tokenizer(nc, t, tok, named)
        blocks(nc, t, tok, out, named)


_INS = ['x', 'L0_tok_fc0_w', 'L0_tok_fc0_b', 'L0_tok_ln0_g', 'L0_tok_ln0_b', 'L0_tok_w1r', 'L0_tok_w1i', 'L0_tok_w2r',
        'L0_tok_w2i', 'L0_tok_conv_w', 'L0_tok_conv_b', 'L0_tok_ln_g', 'L0_tok_ln_b', 'L0_tok_fc1_w', 'L0_tok_fc1_b',
        'L0_tok_fc2_w', 'L0_tok_fc2_b', 'L0_tok_fc3_w', 'L0_tok_fc3_b', 'L0_attn_Wqkv', 'L0_attn_bqkv', 'L0_attn_W0',
        'L0_attn_b0', 'L0_ffn_W1', 'L0_ffn_b1', 'L0_ffn_Wg', 'L0_ffn_bg', 'L0_ffn_Wd', 'L0_ffn_bd', 'L1_attn_E',
        'L1_attn_Dx', 'L1_attn_Dy', 'L1_ffn_Wg', 'L1_ffn_bg', 'L1_ffn_bias', 'L1_ffn_W1', 'L1_ffn_b1', 'L1_ffn_W2',
        'L1_ffn_b2']


def kernel(**inputs):
    import numpy as _np
    import concourse.bacc as _bacc
    from concourse import mybir as _mybir
    from concourse.bass_utils import run_bass_kernel_spmd as _run

    nc = _bacc.Bacc("TRN2", target_bir_lowering=False, num_devices=1)
    arrays, t = {}, {}
    given = {name: _np.ascontiguousarray(inputs[name]) for name in _INS}
    given.update(tables())
    for name, a in given.items():
        arrays[f"in_{name}"] = a
        t[name] = nc.dram_tensor(f"in_{name}", a.shape, _mybir.dt.from_np(a.dtype), kind="ExternalInput").ap()
    out = nc.dram_tensor("out", (IMGS, S, S), F32, kind="ExternalOutput").ap()
    build(nc, t, out)
    r = _run(nc, [arrays], core_ids=[0])
    return r.results[0]["out"]
```

```python
from contextlib import ExitStack

import concourse.bass as bass
from concourse import mybir
import numpy as np

F32 = mybir.dt.float32
I32 = mybir.dt.int32
ALU = mybir.AluOpType
ACT = mybir.ActivationFunctionType
AX = mybir.AxisListType

IMGS, S, CH, CIN = 64, 64, 32, 3
LAYERS, M1, M2 = 4, 12, 12
GROUP, UNITS = 16, 2
GROUPS = IMGS // GROUP
UIMG = GROUP // UNITS
NA, NB = 4, 2
KX = 2 * M1
KP = M2 // 2
STAGES = LAYERS + 1
NCH = S // 4
UCOLS = S * NA * CH
EPS = 1e-5

AX_EMBED, AX_ROWS, AX_A, AX_B, AX_MIX, AX_C = 1, 4, 8, 2, 3, 8
AX_FWD = AX_ROWS + AX_A + AX_B + AX_MIX
AX_MLP = 4
AX_STAGE0 = UNITS * (AX_EMBED + AX_FWD)
AX_LAYER = UNITS * (AX_C + AX_FWD)
AX_LAST = UNITS * AX_C
AX_GROUP = AX_STAGE0 + (LAYERS - 1) * AX_LAYER + AX_LAST + UNITS * AX_MLP

NEWTON_OPS = 9
LAG = 5
CUBIC = 3 / 8
CHUNKS_GROUP = STAGES * UNITS * NCH
START = 1
MLP_BLOCKS = NB * S // 8
FC1_GROUP = UNITS * MLP_BLOCKS * NA
FC2_GROUP = FC1_GROUP // 2
FC1, FC2 = 128, 64
TOK_DMAS = 4 * NB


def dft_tables():
    n = np.arange(S)
    ky = np.arange(M2)
    kx = np.concatenate([np.arange(M1), np.arange(S - M1, S)])
    w_ang = 2 * np.pi * np.outer(n, ky) / S
    r_ang = 2 * np.pi * np.outer(n, kx) / S
    fwd_w = np.zeros((NB, S, NB, 2, M2, 2))
    cos_r = np.zeros((2, S, 2, KX))
    sin_r = np.zeros((2, S, 2, KX))
    for i in range(2):
        fwd_w[i, :, i, 0, :, 0] = np.cos(w_ang)
        fwd_w[i, :, i, 0, :, 1] = -np.sin(w_ang)
        fwd_w[i, :, i, 1, :, 0] = -np.sin(w_ang)
        fwd_w[i, :, i, 1, :, 1] = -np.cos(w_ang)
        cos_r[i, :, i] = np.cos(r_ang)
        sin_r[i, :, i] = np.sin(r_ang)
    weight = np.where(ky == 0, 1.0, 2.0)[:, None] / (S * S)
    inv_w = np.zeros((M2, 2, 4, 4, S))
    for i in range(4):
        inv_w[:, 0, i, i] = weight * np.cos(w_ang.T)
        inv_w[:, 1, i, i] = weight * np.sin(w_ang.T)
    inv_r = np.zeros((2, 2, NB, M1, S, NB))
    for i in range(NB):
        inv_r[0, :, i, :, :, i] = np.cos(r_ang.T).reshape(2, M1, S)
        inv_r[1, :, i, :, :, i] = -np.sin(r_ang.T).reshape(2, M1, S)
    inv_r = np.concatenate([inv_r.reshape(4 * KX, 128), np.ones((1, 128))])
    ident = np.eye(128)
    center = np.eye(CH) - 1.0 / CH
    spread = np.zeros((4, 97))
    mask = np.zeros((97, 8, NA))
    for a in range(NA):
        for w in range(8):
            for c in range(CIN):
                spread[c, a * 24 + w * 3 + c] = 1
                mask[a * 24 + w * 3 + c, w, a] = 1
    spread[3, 96] = 1
    mask[96] = 1
    f = np.float32
    return {
        "t_fwd_w": fwd_w.reshape(128, 96).astype(f), "t_cos_r": cos_r.reshape(128, 48).astype(f),
        "t_sin_r": sin_r.reshape(128, 48).astype(f), "t_inv_w": inv_w.reshape(96, 256).astype(f),
        "t_inv_r": inv_r.astype(f), "t_ident": ident.astype(f), "t_center": center.astype(f),
        "t_spread": spread.astype(f), "t_mask": mask.reshape(97, 32).astype(f),
    }


def tokenizer(nc, t, tok, named):
    ctx = ExitStack()

    def sb(name, shape):
        return ctx.enter_context(nc.sbuf_tensor(name, shape, F32))

    def sem(name):
        return named.enter_context(nc.semaphore(name))

    with ctx:
        mix_scratch = nc.dram_tensor("mix_scratch", (LAYERS, 128, 2 * 2 * M1 * KP * CH), F32, kind="Internal").ap()
        bias_scratch = nc.dram_tensor("bias_scratch", (LAYERS, 16 * NA * CH), F32, kind="Internal").ap()
        embw_scratch = nc.dram_tensor("embw_scratch", (97, 8 * NA * CH), F32, kind="Internal").ap()
        start_scratch = nc.dram_tensor("start_scratch", (2, 16), F32, kind="Internal").ap()
        y_scratch = nc.dram_tensor("y_scratch", (UNITS, 2, M2 * 2 * CH * KX * UIMG), F32, kind="Internal").ap()

        h = sb("h", [128, UNITS * NB * S * S])
        pix = sb("pix", [128, UCOLS])
        mixw = sb("mixw", [128, 2 * 2 * M1 * KP * CH])
        t_w = sb("t_w", [128, 2 * NB * 2 * M2 * 2 * CH])
        XC = KP * KX * 2 * UIMG
        xs = sb("xs", [128, XC + 2 * 2 * UIMG])
        HN = NB * M1 * NA
        ys = t_w[:, 1024:1024 + M2 * HN]
        yn = t_w[:, 1024 + M2 * HN:1024 + 2 * M2 * HN]
        YC = 2 * 8 * KX * UIMG
        yd = sb("yd", [128, UNITS * YC])
        sq = sb("sq", [128, 2, 512])
        xn = sb("xn", [128, 2, 512])
        ssum = sb("ssum", [128, 4, 16])
        var = sb("var", [128, 4, 16])
        rstd = sb("rstd", [128, 4, 16])
        mhalf = sb("mhalf", [128, 16])
        eps = sb("eps", [128, 16])
        newton_w = sb("newton_w", [128, 4, 16])
        start = sb("start", [1, 22])
        fwd_w = sb("fwd_w", [128, 96])
        cos_r = sb("cos_r", [128, 96])
        sin_r = sb("sin_r", [128, 96])
        inv_w = sb("inv_w", [96, 256])
        inv_r = sb("inv_r", [97, 128])
        ident = sb("ident", [128, 128])
        convw = sb("convw", [128, LAYERS, 128])
        gb = sb("gb", [128, 2, STAGES])
        f1w = sb("f1w", [128, NA, FC1])
        f2w = sb("f2w", [128, FC2])
        f3w = sb("f3w", [128, 32])
        fb = sb("fb", [128, 3])

        def xb_of(u):
            return yd[:, u * YC:u * YC + NA * S * CIN]

        def embw_of(u):
            return yd[0:97, u * YC + 2048:u * YC + 3072]

        def xt_of(u):
            return yd[0:97, u * YC + 1024:u * YC + 2048]

        main = [ctx.enter_context(nc.psum_tensor(f"main{i}", [128, 512], F32)) for i in range(4)]
        tp = [ctx.enter_context(nc.psum_tensor(f"tp{i}", [128, 512], F32)) for i in range(2)]
        aux = [ctx.enter_context(nc.psum_tensor(f"aux{i}", [128, 512], F32)) for i in range(2)]
        wide = [*main, *aux]

        p_sum, p_cent, p_neg = (sem(n) for n in ("p_sum", "p_cent", "p_neg"))
        p_store = [sem(f"p_store{i}") for i in range(2)]
        p_raw = [sem(f"p_raw{i}") for i in range(2)]
        p_zero, p_small, p_pe, p_done, p_bias, p_bstore = (
            sem(n) for n in ("p_zero", "p_small", "p_pe", "p_done", "p_bias", "p_bstore"))
        NRAW = CH * M1 * M2
        raw = [[h[:, 0:NRAW], h[:, NRAW:2 * NRAW]], [h[:, 2 * NRAW:3 * NRAW], pix[:, 0:NRAW]]]
        rsum = t_w[:, 0:4 * M1 * M2].rearrange("p (v n) -> p v n", v=4)
        cent = mixw[:, :].rearrange("p (k x y s o) -> p k x y s o", k=2, x=M1, y=KP, s=2)
        cload = xs[0:CH, 0:LAYERS * 128]
        cmat = xs[0:CH, 1024:1056]
        braw = ys[0:1, 0:LAYERS * CH]
        bsum = ys[0:1, 256:256 + LAYERS]
        bcen = ys[0:1, 512:512 + LAYERS * CH]
        eraw = sq[0:4, 0, 0:CH]
        esum = sq[0:4, 0, 64:65]
        ecen = sq[0:4, 0, 128:128 + CH]
        spread = sq[0:4, 0, 256:256 + 97]
        mask = sq[0:97, 1, 0:32]
        with nc.Block() as block:
            @block.sync
            def _(sp):
                sp.wait_ge(p_zero, 5)
                loads = [(fwd_w[:, :], t["t_fwd_w"]), (cos_r[:, 0:48], t["t_cos_r"]), (sin_r[:, 0:48], t["t_sin_r"]),
                         (inv_w[:, :], t["t_inv_w"]), (inv_r[:, :], t["t_inv_r"]), (ident[:, :], t["t_ident"]),
                         (cmat, t["t_center"]), (spread, t["t_spread"]), (mask, t["t_mask"]),
                         (eraw[0:CIN, :], t["L0_tok_fc0_w"]),
                         (eraw[CIN:4, :], t["L0_tok_fc0_b"].rearrange("(a n) -> a n", a=1)),
                         (braw, t["L0_tok_conv_b"].rearrange("(x l) o -> x (l o)", x=1)),
                         (f2w[:, :], t["L0_tok_fc2_w"]),
                         (fb[:, 0:1], t["L0_tok_fc1_b"].rearrange("(n a) -> n a", a=1)),
                         (fb[:, 2:3], t["L0_tok_fc3_b"].rearrange("(n a) -> n a", a=1).to_broadcast([128, 1]))]
                for a in range(NA):
                    rows = slice(32 * a, 32 * a + 32)
                    loads.append((cload.rearrange("o (l a c) -> o l a c", l=LAYERS, a=NA)[:, :, a, :],
                                  t["L0_tok_conv_w"].rearrange("l o c -> o l c")))
                    loads.append((gb[rows, 0, 0:1], t["L0_tok_ln0_g"].rearrange("(n a) -> n a", a=1)))
                    loads.append((gb[rows, 1, 0:1], t["L0_tok_ln0_b"].rearrange("(n a) -> n a", a=1)))
                    for l in range(LAYERS):
                        loads.append((gb[rows, 0, l + 1:l + 2], t["L0_tok_ln_g"][l, :].rearrange("(n a) -> n a", a=1)))
                        loads.append((gb[rows, 1, l + 1:l + 2], t["L0_tok_ln_b"][l, :].rearrange("(n a) -> n a", a=1)))
                    loads.append((f1w[rows, a, :], t["L0_tok_fc1_w"]))
                for i in range(2):
                    rows = slice(64 * i, 64 * i + 64)
                    loads.append((f3w[rows, i:i + 1], t["L0_tok_fc3_w"]))
                    loads.append((fb[rows, 1:2], t["L0_tok_fc2_b"].rearrange("(n a) -> n a", a=1)))
                for dst, src in loads:
                    sp.dma_start(dst, src).then_inc(p_small, 16)
                assert len(loads) == N_SMALL
                sp.wait_ge(p_bias, 2)
                for l in range(LAYERS):
                    sp.dma_start(bias_scratch[l, :].rearrange("(x r o) -> x r o", x=1, o=CH),
                                 bcen[:, l * CH:(l + 1) * CH].unsqueeze(1).to_broadcast([1, 16 * NA, CH])).then_inc(p_bstore, 16)
                sp.wait_ge(p_done, 3)
                sp.dma_start(embw_scratch, embw_of(0)).then_inc(p_bstore, 16)
                sp.wait_ge(p_bstore, 16 * (LAYERS + 1))

            @block.gpsimd
            def _(pool):
                for n in range(LAYERS):
                    dst = mix_scratch[n].rearrange("(k q) (f n) -> q k f n", k=2, f=2)
                    for k in range(2):
                        pool.wait_ge(p_cent, 4 * n + 2 * k + 2)
                        pool.wait_ge(p_neg, 4 * n + 2 * k + 2)
                        for half in range(2):
                            pool.dma_start(dst[:, k, half, :], mixw[64 * half:64 * half + 64, k * NRAW:(k + 1) * NRAW]).then_inc(
                                p_store[k], 16)

            @block.vector
            def _(dve):
                dve.memset(convw[:, :, :], 0.0).then_inc(p_zero, 1)
                dve.memset(f1w[:, :, :], 0.0).then_inc(p_zero, 1)
                dve.memset(f3w[:, :], 0.0).then_inc(p_zero, 1)
                dve.memset(cos_r[:, 48:96], 0.0).then_inc(p_zero, 1)
                dve.memset(sin_r[:, 48:96], 0.0).then_inc(p_zero, 1)
                dve.memset(mhalf[:, :], -0.5)
                dve.memset(eps[:, :], EPS)
                for u in range(UNITS):
                    dve.memset(yd[96:97, u * YC + 1024:u * YC + 2048], 1.0)
                for n in range(LAYERS):
                    dve.wait_ge(p_raw[n % 2], 128 * (n // 2 + 1))
                    for v in range(2):
                        dve.tensor_reduce(rsum[:, 2 * (n % 2) + v, :], raw[n % 2][v].rearrange("p (o n) -> p n o", o=CH), AX.X,
                                          ALU.add).then_inc(p_sum, 1)
                    dve.wait_ge(p_sum, 2 * (n + 1))
                    for k in range(2):
                        if n >= 1:
                            dve.wait_ge(p_store[k], 32 * n)
                        for v in range(2):
                            dve.scalar_tensor_tensor(
                                out=cent[:, k, :, :, v, :],
                                in0=rsum[:, 2 * (n % 2) + v, :].rearrange("p (x y k) -> p x y k", x=M1, k=2)[:, :, :, k].unsqueeze(3).to_broadcast([128, M1, KP, CH]),
                                scalar=-1.0 / CH,
                                in1=raw[n % 2][v].rearrange("p (o x y k) -> p x y o k", o=CH, x=M1, k=2)[:, :, :, :, k],
                                op0=ALU.mult, op1=ALU.add).then_inc(p_cent, 1)
                dve.wait_ge(p_small, 16 * N_SMALL)
                dve.tensor_reduce(bsum, braw.rearrange("p (l o) -> p l o", l=LAYERS), AX.X, ALU.add).then_inc(p_bias, 1)
                dve.wait_ge(p_bias, 1)
                dve.scalar_tensor_tensor(out=bcen.rearrange("p (l o) -> p l o", l=LAYERS),
                                         in0=bsum.unsqueeze(2).to_broadcast([1, LAYERS, CH]), scalar=-1.0 / CH,
                                         in1=braw.rearrange("p (l o) -> p l o", l=LAYERS),
                                         op0=ALU.mult, op1=ALU.add).then_inc(p_bias, 1)
                dve.tensor_reduce(esum, eraw, AX.X, ALU.add).then_inc(p_done, 1)
                dve.wait_ge(p_done, 1)
                dve.scalar_tensor_tensor(out=ecen, in0=esum.to_broadcast([4, CH]), scalar=-1.0 / CH, in1=eraw,
                                         op0=ALU.mult, op1=ALU.add).then_inc(p_done, 1)
                dve.wait_ge(p_pe, 1)
                dve.tensor_tensor(embw_of(0).rearrange("p (m o) -> p m o", o=CH),
                                  mask.unsqueeze(2).to_broadcast([97, 32, CH]),
                                  aux[0][0:97, 0:CH].unsqueeze(1).to_broadcast([97, 32, CH]), ALU.mult).then_inc(p_done, 1)
                dve.wait_ge(p_pe, 2)
                for l in range(LAYERS):
                    for a in range(NA):
                        dve.tensor_copy(convw[32 * a:32 * a + 32, l, 32 * a:32 * a + 32],
                                        aux[1][32 * a:32 * a + 32, 32 * l:32 * l + 32])

            @block.scalar
            def _(act):
                def load(n):
                    for q, names in enumerate((("w1r", "w1i"), ("w1i", "w1r"), ("w2r", "w2i"), ("w2i", "w2r"))):
                        for v in range(2):
                            act.dma_start(raw[n % 2][v][32 * q:32 * q + 32, :],
                                          t["L0_tok_" + names[v]][n].rearrange("i o x y -> i (o x y)")).then_inc(p_raw[n % 2], 16)

                load(0)
                for n in range(LAYERS):
                    if n + 1 < LAYERS:
                        if n >= 1:
                            act.wait_ge(p_cent, 4 * n)
                        load(n + 1)
                    for k in range(2):
                        act.wait_ge(p_cent, 4 * n + 2 * k + 1)
                        for q in (32, 96):
                            v = mixw[q:q + 32, k * NRAW:(k + 1) * NRAW].rearrange("p (n s o) -> p n s o", s=2, o=CH)[:, :, 0, :]
                            act.mul(v, v, -1.0).then_inc(p_neg, 1)

            @block.tensor
            def _(pe):
                pe.wait_ge(p_small, 16 * N_SMALL)
                pe.wait_ge(p_done, 2)
                pe.matmul(aux[0][0:97, 0:CH], spread, ecen, start=True, stop=True).then_inc(p_pe, 1)
                for l in range(LAYERS):
                    mm = pe.matmul(aux[1][:, 32 * l:32 * l + 32], cload[:, 128 * l:128 * l + 128], cmat,
                                   start=True, stop=True)
                mm.then_inc(p_pe, 1)

        main_full, main_free, sq_full, red_done, var_done, rstd_done, newton, tp_full, tp_free = (
            sem(n) for n in ("main_full", "main_free", "sq_full", "red_done", "var_done", "rstd_done", "newton",
                                  "tp_full", "tp_free"))
        aux_full = [sem(f"aux_full{i}") for i in range(2)]
        aux_free = [sem(f"aux_free{i}") for i in range(2)]
        row_full = [sem(f"row_full{i}") for i in range(2)]
        row_free = [sem(f"row_free{i}") for i in range(2)]
        bias_in, mixw_in, xs_zero, y_ready, y_stored = (
            sem(n) for n in ("bias_in", "mixw_in", "xs_zero", "y_ready", "y_stored"))
        x_in = [sem(f"x_in{u}") for u in range(UNITS)]
        yd_in = [sem(f"yd_in{u}") for u in range(UNITS)]
        fc1_full, g1_done, fc2_full, g2_done, tok_out = (
            sem(n) for n in ("fc1_full", "g1_done", "fc2_full", "g2_done", "tok_out"))

        hv = h[:, :].rearrange("p (u n w) -> p u n w", u=UNITS, w=S)
        pv = pix[:, :].rearrange("p (c a r) -> p c a r", r=S, a=NA)
        qv = pix[0:97, :].rearrange("p (w a c) -> p w a c", w=S, a=NA)
        tv = t_w[:, :].rearrange("p (j b v k s c) -> p j b v k s c", j=2, b=NB, v=2, k=M2, s=2)
        mv = mixw[:, :].rearrange("p (x y n) -> p x y n", x=KX, y=KP)
        xv = xs[:, 0:XC].rearrange("p (y x k b a) -> p y x k b a", y=KP, x=KX, k=2, b=NB)
        yv = ys.rearrange("p (y m x a) -> p y m x a", y=KP, m=2 * NB, x=M1)
        ydv = yd[0:96, :].rearrange("p (u o n a) -> p u o n a", u=UNITS, o=8, a=NA)
        g1 = pix[:, 0:4 * 512].rearrange("p (j n) -> p j n", j=4)
        g2 = pix[:, 4 * 512:8 * 512].rearrange("p (j n) -> p j n", j=4)

        def tok_of(u):
            return (pix[:, 4096:8192] if u == 0 else t_w[:, 0:4096]).rearrange("p (k r b w) -> p k r b w", k=8, r=4, b=NB)


        def base_of(g, s, u, l=None):
            if l is not None:
                return (g * CHUNKS_GROUP + l * (UNITS * NCH) + (START + (UNITS + u) * NCH),
                        g * AX_GROUP + l * AX_LAYER + (START + AX_STAGE0 + u * (AX_LAYER // 2)))
            chunks = g * CHUNKS_GROUP + (START + (s * UNITS + u) * NCH)
            if s == 0:
                return chunks, g * AX_GROUP + (START + u * (AX_STAGE0 // 2))
            done = AX_STAGE0 + (s - 1) * AX_LAYER
            return chunks, g * AX_GROUP + (START + done + u * (AX_C if s == LAYERS else AX_LAYER // 2))

        def after(n, c, depth):
            return n + max(0, c - depth + 1)

        def pe_aux(pe, j, n):
            pe.wait_ge(aux_free[j], n)

        def pe_embed(pe, g, u):
            _, n = base_of(g, 0, u)
            pe.wait_ge(x_in[u], (g + 1) * ((UIMG + 1) * 16))
            for j in range(2):
                pe_aux(pe, j, n)
                for i in range(4):
                    o = (4 * j + i) * 96
                    mm = pe.transpose(aux[j][0:96, 128 * i:128 * i + 128], xb_of(u)[:, o:o + 96], ident[:, :])
                mm.then_inc(aux_full[j], 1)
            for j in range(2):
                pe.wait_ge(aux_free[j], n + 1)

        def pe_inverse(pe, g, s, u, l):
            _, n = base_of(g, s, u, l)
            stage = l if l is not None else s - 1
            pe.wait_ge(yd_in[u], (g * LAYERS + stage + 1) * 32)
            for k in range(2 * AX_C):
                j, a, o = k % 2, k // 4, 2 * (k % 4)
                pe_aux(pe, j, n + k // 2)
                for i in range(2):
                    mm = pe.matmul(aux[j][0:96, 256 * i:256 * i + 256], ydv[:, u, o + i, :, a],
                                   inv_w[:, :], start=True, stop=True)
                mm.then_inc(aux_full[j], 1)
            for j in range(2):
                pe.wait_ge(aux_free[j], n + AX_C)
            pe.wait_ge(bias_in, (g * (LAYERS * UNITS) + stage * UNITS + (u + 1)) * 16)

        def pe_main(pe, g, s, u, l):
            m, _ = base_of(g, s, u, l)
            layer = l if l is not None else s - 1
            for c in range(NCH + LAG):
                if c < NCH:
                    bank = wide[c % 6]
                    pe.wait_ge(main_free, after(m, c, 6))
                    if s == 0:
                        mm = pe.matmul(bank[:, :], xt_of(u)[:, 128 * (c // 2):128 * (c // 2) + 128],
                                       embw_of(u)[:, 512 * (c % 2):512 * (c % 2) + 512], start=True, stop=True)
                    else:
                        pe.matmul(bank[:, :], inv_r[:, :], pix[0:97, 512 * c:512 * c + 512], start=True, stop=False)
                        for i in range(4):
                            mm = pe.matmul(bank[:, 128 * i:128 * i + 128], hv[:, u, :, 4 * c + i],
                                           convw[:, layer, :] if l is None else convw[:, bass.ds(layer, 1), :], start=False, stop=(i == 3))
                    mm.then_inc(main_full, 1)
                if c >= LAG:
                    d = c - LAG
                    pe.wait_ge(main_free, m + d + 1)
                    pe.wait_ge(tp_free, after(m, d, 2))
                    for i in range(4):
                        mm = pe.transpose(tp[d % 2][:, 128 * i:128 * i + 128], xn[:, d % 2, 128 * i:128 * i + 128],
                                          ident[:, :])
                    mm.then_inc(tp_full, 1)

        def pe_forward(pe, g, s, u, l):
            m, n = base_of(g, s, u, l)
            n = n + (AX_EMBED if s == 0 else AX_C)
            pe.wait_ge(tp_free, m + NCH)
            rows = (g * (LAYERS * UNITS) + (0 if s == 0 else l * UNITS + UNITS) + u) * AX_ROWS + START
            for k in range(4 * AX_ROWS):
                j, first = k % 2, k % 4 < 2
                if first:
                    pe_aux(pe, j, n + k // 4)
                else:
                    pe.wait_ge(row_free[j], rows + k // 4)
                for i in range(4):
                    mm = pe.transpose((aux if first else tp)[j][:, 128 * i:128 * i + 128],
                                      h[:, (u * S + 4 * k + i) * 128:(u * S + 4 * k + i) * 128 + 128], ident[:, :])
                mm.then_inc(aux_full[j] if first else row_full[j], 1)
            n = n + AX_ROWS
            for j in range(2):
                pe.wait_ge(aux_free[j], n)
                pe.wait_ge(row_free[j], rows + AX_ROWS)
            for k in range(2 * AX_A):
                j, ap, c0 = k % 2, k // 8, 4 * (k % 8)
                pe_aux(pe, j, n + k // 2)
                for i in range(4):
                    mm = pe.matmul(aux[j][:, 96 * i:96 * i + 96],
                                   pv[:, c0 + i, 2 * ap:2 * ap + 2, :].rearrange("p a r -> p (a r)"),
                                   fwd_w[:, :], start=True, stop=True)
                mm.then_inc(aux_full[j], 1)
            n = n + AX_A
            for j in range(2):
                pe.wait_ge(aux_free[j], n)
            if u == 0:
                pe.wait_ge(mixw_in, (g * LAYERS + (0 if s == 0 else (l + 1)) + 1) * 16)
            for k in range(2 * AX_B):
                j, ap, b = k % 2, k // 2, k % 2
                pe_aux(pe, j, n + k // 2)
                for y in range(KP):
                    o = aux[j][:, 48 * y:48 * y + 96]
                    for v, table in enumerate((cos_r, sin_r)):
                        mm = pe.matmul(o, tv[:, ap, b, v, 2 * y:2 * y + 2].rearrange("p k s c -> p (k s c)"), table[:, :],
                                       start=(v == 0), stop=(v == 1), skip_group_check=True)
                mm.then_inc(aux_full[j], 1)
            n = n + AX_B
            for j in range(2):
                pe.wait_ge(aux_free[j], n)
            for y in range(2 * AX_MIX):
                j = y % 2
                pe_aux(pe, j, n + y // 2)
                for x in range(M1):
                    for half in range(2):
                        at = ((y * KX + half * M1 + x) * 2) * UIMG
                        mm = pe.matmul(aux[j][64 * half:64 * half + 64, 16 * x:16 * x + 48],
                                       mv[:, half * M1 + x, y, :], xs[:, at:at + 48],
                                       start=True, stop=True, skip_group_check=True)
                mm.then_inc(aux_full[j], 1)

        def pe_mlp(pe, g, u):
            n = g * AX_GROUP + (START + AX_GROUP - (UNITS - u) * AX_MLP)
            f1 = g * FC1_GROUP + (START + u * (FC1_GROUP // 2))
            f2 = g * FC2_GROUP + (START + u * (FC2_GROUP // 2))
            if u == 0:
                pe.wait_ge(main_free, g * CHUNKS_GROUP + (START + CHUNKS_GROUP))
                pe.wait_ge(tp_free, g * CHUNKS_GROUP + (START + CHUNKS_GROUP))
            total = MLP_BLOCKS * NA
            hb = h[:, :].rearrange("p (u k n) -> p u k n", u=UNITS, n=512)
            for i in range(total + 6):
                if i < total:
                    k, a = i // NA, i % NA
                    pe.wait_ge(g1_done, after(f1, i, 4))
                    pe.matmul(main[i % 4][:, :], f1w[:, a, :], hb[:, u, k, :], start=True, stop=True).then_inc(fc1_full, 1)
                if 2 <= i < total + 2:
                    d = i - 2
                    pe.wait_ge(g1_done, f1 + d + 1)
                    if d % 2 == 0:
                        pe.wait_ge(g2_done, after(f2, d // 2, 2))
                    mm = pe.matmul(tp[d // 2 % 2][64 * (d % 2):64 * (d % 2) + 64, :], f2w[:, :], g1[:, d % 4, :],
                                   start=True, stop=True)
                    if d % 2:
                        mm.then_inc(fc2_full, 1)
                if i >= 6 and i % 2 == 0:
                    d = (i - 6) // 2
                    j = d // 4 % 2
                    if d % 4 == 0:
                        pe_aux(pe, j, n + d // 8)
                    pe.wait_ge(g2_done, f2 + d + 1)
                    mm = pe.matmul(aux[j][32 * (d % 4):32 * (d % 4) + 32, :], f3w[:, :], g2[:, d % 4, :], start=True, stop=True)
                    if d % 4 == 3:
                        mm.then_inc(aux_full[j], 1)

        def copy(eng, j, out, in_):
            return eng.tensor_copy(out, in_) if j == 0 else eng.copy(out, in_)

        def drain_embed(eng, j, g, u):
            _, n = base_of(g, 0, u)
            if u == 0:
                eng.wait_ge(tok_out, g * (UNITS * TOK_DMAS * 16) + 16)
            eng.wait_ge(aux_full[j], n + 1)
            copy(eng, j, xt_of(u)[0:96, 512 * j:512 * j + 512], aux[j][0:96, :]).then_inc(aux_free[j], 1)

        def drain_inverse(eng, j, g, s, u, l):
            _, n = base_of(g, s, u, l)
            for k in range(j, 2 * AX_C, 2):
                a, o = k // 4, 2 * (k % 4)
                eng.wait_ge(aux_full[j], n + (k // 2 + 1))
                out = qv[0:96, :, a, :].rearrange("p w (d e) -> p e d w", d=4)[:, o:o + 2]
                copy(eng, j, out, aux[j][0:96, :].rearrange("p (e d w) -> p e d w", e=2, d=4)).then_inc(aux_free[j], 1)

        def drain_forward(eng, j, g, s, u, l):
            _, n = base_of(g, s, u, l)
            n = n + (AX_EMBED if s == 0 else AX_C)
            fwd = (g * (LAYERS * UNITS) + (0 if s == 0 else l * UNITS + UNITS) + u)
            for k in range(j, 4 * AX_ROWS, 2):
                first = k % 4 < 2
                if first:
                    eng.wait_ge(aux_full[j], n + (k // 4 + 1))
                else:
                    eng.wait_ge(row_full[j], fwd * AX_ROWS + (START + k // 4 + 1))
                copy(eng, j, pv[:, :, :, 4 * k:4 * k + 4].rearrange("p c a r -> p a c r"),
                     (aux if first else tp)[j][:, :].rearrange("p (r a c) -> p a c r", r=4, a=NA)).then_inc(
                         aux_free[j] if first else row_free[j], 1)
            n = n + AX_ROWS
            eng.wait_ge(y_stored, fwd * 128 + 16)
            for k in range(j, 2 * AX_A, 2):
                ap, c0 = k // 8, 4 * (k % 8)
                eng.wait_ge(aux_full[j], n + (k // 2 + 1))
                out = tv[:, ap, :, :, :, :, c0:c0 + 4].rearrange("p b v k s c -> p (b v k s) c")
                copy(eng, j, out, aux[j][:, 0:384].rearrange("p (c n) -> p n c", c=4)).then_inc(aux_free[j], 1)
            n = n + AX_A
            for k in range(j, 2 * AX_B, 2):
                ap, b = k // 2, k % 2
                eng.wait_ge(aux_full[j], n + (k // 2 + 1))
                for ky in range(2):
                    rows = slice(64 * ky, 64 * ky + 64)
                    out = xv[rows, :, :, ky, b, 2 * ap:2 * ap + 2].rearrange("p y x a -> p y a x")
                    ins = copy(eng, j, out, aux[j][rows, 0:288].rearrange("p (y a x) -> p y a x", y=KP, a=2))
                ins.then_inc(aux_free[j], 1)
            n = n + AX_B
            for k in range(j, 2 * AX_MIX, 2):
                eng.wait_ge(aux_full[j], n + (k // 2 + 1))
                copy(eng, j, yv[:, k], aux[j][:, 0:192].rearrange("p (x m a) -> p m x a", m=2 * NB, a=NA)).then_inc(aux_free[j], 1)
            if j == 0:
                eng.wait_ge(aux_free[0], n + AX_MIX)
                eng.wait_ge(aux_free[1], n + AX_MIX)
                eng.tensor_scalar(yn, ys, -1.0, None, ALU.mult).then_inc(y_ready, 1)

        def dve_newton(dve, m, c):
            v, y, w = (x[:, 2:4, :].rearrange("p k n -> p (k n)") for x in (var, rstd, newton_w))
            done = (m - START) * NEWTON_OPS + (START + (c // 4) * 4 * NEWTON_OPS)
            dve.wait_ge(red_done, m + c + 1)
            dve.tensor_scalar(v, ssum[:, 2:4, :].rearrange("p k n -> p (k n)"), EPS / CUBIC ** 2, None, ALU.add).then_inc(newton, 4)
            dve.wait_ge(main_free, after(m, c, 4))
            dve.wait_ge(newton, done + 4)
            dve.tensor_scalar(y.bitcast(I32), v.bitcast(I32), -0.5, float(0x5f3759df), ALU.mult, ALU.add).then_inc(newton, 4)
            dve.wait_ge(newton, done + 8)
            dve.tensor_tensor(w, y, y, ALU.mult).then_inc(newton, 4)
            dve.wait_ge(newton, done + 12)
            dve.tensor_tensor(w, w, v, ALU.mult).then_inc(newton, 4)
            dve.wait_ge(newton, done + 16)
            dve.scalar_tensor_tensor(out=w, in0=w, scalar=-10 / 3, in1=w, op0=ALU.add, op1=ALU.mult).then_inc(newton, 4)
            dve.wait_ge(newton, done + 20)
            dve.scalar_tensor_tensor(out=y, in0=w, scalar=5.0, in1=y, op0=ALU.add, op1=ALU.mult).then_inc(newton, 4)
            dve.wait_ge(newton, done + 24)
            dve.scalar_tensor_tensor(out=w, in0=y, scalar=-0.5 * CUBIC ** 2, in1=y, op0=ALU.mult, op1=ALU.mult).then_inc(newton, 4)
            dve.wait_ge(newton, done + 28)
            dve.tensor_tensor(w, w, v, ALU.mult).then_inc(newton, 4)
            dve.wait_ge(newton, done + 32)
            dve.scalar_tensor_tensor(out=y, in0=w, scalar=1.5, in1=y, op0=ALU.add, op1=ALU.mult).then_inc(newton, 4)

        def wait_rstd(dve, m, c):
            if c % 4 < 2:
                dve.wait_ge(rstd_done, m + 4 * (c // 4) + 2 * (c % 4 + 1))
            else:
                dve.wait_ge(newton, (m - START) * NEWTON_OPS + (START + (c // 4 + 1) * 4 * NEWTON_OPS))

        def dve_main(dve, g, s, u, l):
            m, _ = base_of(g, s, u, l)

            def scale(d):
                wait_rstd(dve, m, d)
                dve.wait_ge(tp_full, after(m, d, 2))
                dve.tensor_tensor(xn[:, d % 2, :].rearrange("p (n c) -> p n c", c=CH),
                                  wide[d % 6][:, :].rearrange("p (n c) -> p n c", c=CH),
                                  rstd[:, d % 4, :].unsqueeze(2).to_broadcast([128, 16, CH]),
                                  ALU.mult).then_inc(main_free, 1)

            for c in range(NCH):
                dve.wait_ge(sq_full, m + c + 1)
                if c >= 4:
                    wait_rstd(dve, m, c - 4)
                dve.tensor_reduce(ssum[:, c % 4, :], sq[:, c % 2, :].rearrange("p (n c) -> p n c", c=CH), AX.X,
                                  ALU.add).then_inc(red_done, 1)
                if c >= 3:
                    scale(c - 3)
                if c % 4 == 3:
                    dve_newton(dve, m, c)
            for d in range(NCH - 3, NCH):
                scale(d)

        def act_main(act, g, s, u, l):
            m, _ = base_of(g, s, u, l)
            stage = l + 1 if l is not None else s
            fn = ACT.Identity if s in (0, LAYERS) else ACT.Gelu
            for c in range(NCH + LAG):
                if c < NCH:
                    act.wait_ge(main_full, m + c + 1)
                    act.wait_ge(red_done, after(m, c, 2))
                    act.activation(sq[:, c % 2, :], wide[c % 6][:, :], ACT.Square,
                                   scale=CH ** -0.5 / (CUBIC if c % 4 >= 2 else 1)).then_inc(sq_full, 1)
                if c >= LAG:
                    d = c - LAG
                    act.wait_ge(p_small, 16 * N_SMALL)
                    act.wait_ge(tp_full, m + d + 1)
                    act.activation(hv[:, u, :, 4 * d:4 * d + 4].rearrange("p n w -> p w n"),
                                   tp[d % 2][:, :].rearrange("p (w n) -> p w n", w=4), fn,
                                   bias=gb[:, 1, stage:stage + 1] if l is None else gb[:, 1, bass.ds(stage, 1)],
                                   scale=gb[:, 0, stage:stage + 1] if l is None else gb[:, 0, bass.ds(stage, 1)]).then_inc(tp_free, 1)

        def pool_main(pool, g, s, u, l):
            m, _ = base_of(g, s, u, l)
            for c in range(NCH):
                if c % 4 < 2:
                    pool.wait_ge(red_done, m + c + 1)
                    pool.tensor_tensor(var[:, c % 4, :], ssum[:, c % 4, :], eps[:, :], ALU.add).then_inc(var_done, 2)
                    pool.wait_ge(var_done, m + 4 * (c // 4) + 2 * (c % 4 + 1))
                    pool.wait_ge(main_free, after(m, c, 4))
                    pool.tensor_tensor(rstd[:, c % 4, :], var[:, c % 4, :], mhalf[:, :], ALU.pow).then_inc(rstd_done, 2)

        def act_mlp(act, g, u):
            n = g * AX_GROUP + (START + AX_GROUP - (UNITS - u) * AX_MLP)
            f1 = g * FC1_GROUP + (START + u * (FC1_GROUP // 2))
            f2 = g * FC2_GROUP + (START + u * (FC2_GROUP // 2))
            for i in range(MLP_BLOCKS * NA + 3):
                if i < MLP_BLOCKS * NA:
                    act.wait_ge(fc1_full, f1 + i + 1)
                    if i >= 4:
                        act.wait_ge(fc2_full, f2 + (i - 2) // 2)
                    act.activation(g1[:, i % 4, :], main[i % 4][:, :], ACT.Gelu, bias=fb[:, 0:1]).then_inc(g1_done, 1)
                if i >= 3 and i % 2 == 1:
                    d = (i - 3) // 2
                    act.wait_ge(fc2_full, f2 + d + 1)
                    if d >= 4:
                        act.wait_ge(fc1_full, f1 + min(MLP_BLOCKS * NA, 2 * (d - 4) + 8))
                    act.activation(g2[:, d % 4, :], tp[d % 2][:, :], ACT.Gelu, bias=fb[:, 1:2]).then_inc(g2_done, 1)

        def dve_mlp(dve, g, u):
            n = g * AX_GROUP + (START + AX_GROUP - (UNITS - u) * AX_MLP)
            for k in range(2 * AX_MLP):
                j = k % 2
                dve.wait_ge(aux_full[j], n + (k // 2 + 1))
                dve.tensor_scalar(tok_of(u)[:, k].rearrange("p r b w -> p (r b w)"), aux[j][:, :], fb[:, 2:3], None,
                                  ALU.add).then_inc(aux_free[j], 1)

        def sp_x(sp, g, u):
            for b in range(NB):
                for a in range(NA):
                    img = g * GROUP + (u * UIMG + b * NA + a)
                    sp.dma_start(xb_of(u)[b:128:2, :].rearrange("r (k a n) -> r a k n", k=8, a=NA)[:, a],
                                 t["x"][bass.ds(img, 1)].rearrange("a r (k w) c -> r (a k) (w c)", k=8)).then_inc(x_in[u], 16)

            sp.dma_start(embw_of(u), embw_scratch).then_inc(x_in[u], 16)

        def sp_bias(sp, g, s, u, l):
            _, n = base_of(g, s, u, l)
            layer = l if l is not None else s - 1
            if s == LAYERS and u == 1:
                sp.wait_ge(main_full, g * CHUNKS_GROUP + (START + (LAYERS * UNITS + 1) * NCH))
            else:
                sp.wait_ge(aux_full[1], n - (AX_B + AX_MIX))
            sp.dma_start(pix[96:97, :].rearrange("p (k n) -> p k n", k=4),
                         bias_scratch[bass.ds(layer, 1), :].unsqueeze(1).to_broadcast([1, 4, 16 * NA * CH])).then_inc(bias_in, 16)

        def sp_spectrum(sp, g, s, u, l):
            fwd = (g * (LAYERS * UNITS) + (0 if s == 0 else l * UNITS + UNITS) + u)
            sp.wait_ge(y_ready, fwd + 1)
            for half in range(2):
                for ro, ri, src in ((0, 0, ys), (0, 1, yn), (1, 0, ys), (1, 1, ys)):
                    part = ri if ro == 0 else 1 - ri
                    rows = 64 * half + 32 * part
                    dst = y_scratch[u, ro].rearrange("(y r o f n) -> o y r f n", y=M2, r=2, o=CH, f=2)[:, :, ri, half, :]
                    sp.dma_start(dst, src[rows:rows + 32, :].rearrange("o (y n) -> o y n", y=M2)).then_inc(y_stored, 16)
            sp.wait_ge(y_stored, fwd * 128 + 144)
            for ro in range(2):
                sp.dma_start(yd[0:96, u * YC:(u + 1) * YC].rearrange("p (e s n) -> p e s n", e=8, s=2)[:, :, ro],
                             y_scratch[u, ro].rearrange("(p e n) -> p e n", p=96, e=8)).then_inc(yd_in[u], 16)

        def sp_mixw(sp, layer):
            sp.dma_start(mixw[:, :], mix_scratch[bass.ds(layer, 1)].rearrange("a p n -> (a p) n")).then_inc(mixw_in, 16)

        def sp_tok(sp, g, u):
            n = g * AX_GROUP + (START + AX_GROUP - (UNITS - u) * AX_MLP)
            for j in range(2):
                sp.wait_ge(aux_free[j], n + AX_MLP)
            for q in range(4):
                for b in range(NB):
                    k2, ap = q // 2, q % 2
                    img = g * GROUP + (u * UIMG + b * NA + 2 * ap)
                    sp.dma_start(tok[bass.ds(img, 2)].rearrange("i (k q r) w -> q i k r w", q=2, r=4)[k2],
                                 tok_of(u)[32 * q:32 * q + 2, :, :, b, :]).then_inc(tok_out, 16)

        def program(eng, embed, layer, last, mlp):
            with eng.Fori(0, GROUPS) as g:
                embed(g)
                with eng.Fori(0, LAYERS - 1) as l:
                    layer(g, l)
                last(g)
                mlp(g)

        with nc.Block() as block:
            @block.tensor
            def _(pe):
                def embed(g):
                    for u in range(UNITS):
                        pe_embed(pe, g, u)
                        pe_main(pe, g, 0, u, None)
                        pe_forward(pe, g, 0, u, None)

                def layer(g, l):
                    for u in range(UNITS):
                        pe_inverse(pe, g, 1, u, l)
                        pe_main(pe, g, 1, u, l)
                        pe_forward(pe, g, 1, u, l)

                def last(g):
                    for u in range(UNITS):
                        pe_inverse(pe, g, LAYERS, u, None)
                        pe_main(pe, g, LAYERS, u, None)

                def mlp(g):
                    for u in range(UNITS):
                        pe_mlp(pe, g, u)

                program(pe, embed, layer, last, mlp)

            def drains(eng, j, main_of, mlp_of):
                def embed(g):
                    for u in range(UNITS):
                        drain_embed(eng, j, g, u)
                        main_of(eng, g, 0, u, None)
                        drain_forward(eng, j, g, 0, u, None)

                def layer(g, l):
                    for u in range(UNITS):
                        drain_inverse(eng, j, g, 1, u, l)
                        main_of(eng, g, 1, u, l)
                        drain_forward(eng, j, g, 1, u, l)

                def last(g):
                    for u in range(UNITS):
                        drain_inverse(eng, j, g, LAYERS, u, None)
                        main_of(eng, g, LAYERS, u, None)

                def mlp(g):
                    for u in range(UNITS):
                        mlp_of(eng, g, u)

                program(eng, embed, layer, last, mlp)

            @block.vector
            def _(dve):
                dve.memset(xs[:, :], 0.0).then_inc(xs_zero, 1)
                for i, counter in enumerate((*aux_full, *aux_free, *row_full, *row_free, main_full, main_free, sq_full, red_done, var_done, rstd_done, newton,
                                             tp_full, tp_free, fc1_full, g1_done, fc2_full, g2_done)):
                    dve.memset(start[:, i:i + 1], 0.0).then_inc(counter, START)
                dve.wait_ge(xs_zero, 1)
                drains(dve, 0, dve_main, dve_mlp)

            @block.scalar
            def _(act):
                for k in range(2):
                    act.wait_ge(p_store[k], 32 * LAYERS)
                act.dma_start(mixw[:, :], mix_scratch[0]).then_inc(mixw_in, 16)
                act.wait_ge(xs_zero, 1)
                drains(act, 1, act_main, act_mlp)

            @block.gpsimd
            def _(pool):
                def one(s):
                    def f(g, l=None):
                        for u in range(UNITS):
                            pool_main(pool, g, s, u, l)
                    return f
                program(pool, one(0), one(1), one(LAYERS), lambda g: None)

            @block.sync
            def _(sp):
                sp.dma_start(start_scratch[0:1, :], eps[0:1, :]).then_inc(y_stored, 16)
                sp.dma_start(start_scratch[1:2, :], eps[0:1, :]).then_inc(tok_out, 16)
                with sp.Fori(0, GROUPS) as g:
                    sp.wait_ge(main_full, g * CHUNKS_GROUP + START)
                    for u in range(UNITS):
                        sp_x(sp, g, u)
                    for u in range(UNITS):
                        sp_spectrum(sp, g, 0, u, None)
                    with sp.Fori(0, LAYERS - 1) as l:
                        for u in range(UNITS):
                            sp_bias(sp, g, 1, u, l)
                            if u == 0:
                                sp_mixw(sp, l + 1)
                            sp_spectrum(sp, g, 1, u, l)
                    for u in range(UNITS):
                        sp_bias(sp, g, LAYERS, u, None)
                        if u == 0:
                            sp_mixw(sp, 0)
                    for u in range(UNITS):
                        sp_tok(sp, g, u)
                sp.wait_ge(tok_out, GROUPS * UNITS * TOK_DMAS * 16 + 16)
                sp.wait_ge(mixw_in, (GROUPS * LAYERS + 1) * 16)


N_SMALL = 15 + NA * (1 + 2 + 2 * LAYERS + 1) + 4


TOK, D = IMGS * S, S
NT = TOK // 128
HEADS = 8
HP = HEADS // 2
QW = D * HEADS
HID, NE = 256, 8
NST = 256
ED = 128
DECAY, L1_EPS = 0.97, 1e-12
PADN = 96


def block_tables():
    f = np.float32
    s, q = np.meshgrid(np.arange(S), np.arange(S), indexing="ij")
    decay = np.where(s < q, DECAY ** np.maximum(q - 1 - s, 0), 0.0)
    return {
        "t_decay": np.concatenate([decay, decay]).astype(f),
        "t_diag": np.concatenate([np.eye(S)] * 2).astype(f),
        "t_rank": np.tile(np.arange(NE, 0, -1), (128, 1)).astype(f),
    }


def tables():
    return {**dft_tables(), **block_tables()}


def blocks(nc, t, tok, out, named):
    ctx = ExitStack()

    def sb(name, shape):
        return ctx.enter_context(nc.sbuf_tensor(name, shape, F32))

    def sems(tag, *names):
        return [named.enter_context(nc.semaphore(f"{tag}_{n}")) for n in names]

    with ctx:
        hid = sb("hid", [128, NT, D])
        z = sb("z", [128, NT, D])
        lv = sb("lv", [128, NT, D])
        zt = sb("zt", [128, TOK])
        big = sb("big", [128, 2, 4 * TOK])
        stat = sb("stat", [128, 6, NT])
        nhalf = sb("nhalf", [128, NT])
        ident = sb("ident2", [128, 128])
        wqkv = sb("wqkv", [128, 3 * QW])
        w0 = sb("w0", [128, HP, 2 * D])
        b0 = sb("b0", [128, D])
        w1 = sb("w1", [128, HID])
        wd = sb("wd", [128, 2, NE * D])
        wg = sb("wg", [128, 2, PADN])
        bd = sb("bd", [128, NE * D])
        bg = sb("bg", [128, NE])
        dxt = sb("dxt", [128, NST])
        dyt = sb("dyt", [128, NST])
        et = sb("et", [128, 2, PADN])
        decay = sb("decay", [128, S])
        diag = sb("diag", [128, S])
        rank = sb("rank", [128, NE])
        ones = sb("ones", [128, 128])
        gates = sb("gates", [128, 8, NT * NE])
        attn = gates[:, 0, :].rearrange("p (i e) -> p i e", e=NE)
        x1 = sb("x1w", [128, NE * ED])
        x2 = sb("x2w", [128, NE, D])
        xg = sb("xg", [128, PADN])
        x2b = sb("x2b", [128, NE * D])
        ps = [ctx.enter_context(nc.psum_tensor(f"bank{i}", [128, 512], F32)) for i in range(8)]
        raww = big[0:64, 1, 0:3 * QW]
        rawd = big[:, 1, 2048:2048 + 4 * D].rearrange("p (k n) -> p k n", n=D)
        rawe = big[0:64, 1, 2560:2560 + NST]

        w_zero, w_in, w_pe = sems("w", "zero", "in", "pe")
        loads = [(ident[:, :], t["t_ident"]), (decay[:, :], t["t_decay"]), (diag[:, :], t["t_diag"]),
                 (rank[:, :], t["t_rank"]), (raww, t["L0_attn_Wqkv"]),
                 (big[64:65, 1, 0:3 * QW], t["L0_attn_bqkv"].rearrange("(a n) -> a n", a=1)),
                 (b0[:, :], t["L0_attn_b0"].rearrange("(a n) -> a n", a=1).to_broadcast([128, D])),
                 (w1[0:D, :], t["L0_ffn_W1"]), (w1[D:D + 1, :], t["L0_ffn_b1"].rearrange("(a n) -> a n", a=1)),
                 (bd[:, :], t["L0_ffn_bd"].rearrange("(a e) n -> a (e n)", a=1).to_broadcast([128, NE * D])),
                 (bg[:, :], t["L0_ffn_bg"].rearrange("(a n) -> a n", a=1).to_broadcast([128, NE])),
                 (rawe, t["L1_attn_E"]),
                 (rawd[:, 0:2, :], t["L1_attn_Dx"].rearrange("(k p) d -> p k d", p=128)),
                 (rawd[:, 2:4, :], t["L1_attn_Dy"].rearrange("(k p) d -> p k d", p=128)),
                 (x1[0:D, :].rearrange("p (e n) -> p e n", e=NE), t["L1_ffn_W1"].rearrange("e d n -> d e n")),
                 (x1[D:D + 1, :], t["L1_ffn_b1"].rearrange("(a e) n -> a (e n)", a=1)),
                 (x2[:, :, :], t["L1_ffn_W2"].rearrange("e p n -> p e n")),
                 (x2b[:, :], t["L1_ffn_b2"].rearrange("(a e) n -> a (e n)", a=1).to_broadcast([128, NE * D])),
                 (xg[0:D, 0:NE], t["L1_ffn_Wg"]), (xg[D:D + 1, 0:NE], t["L1_ffn_bg"].rearrange("(a n) -> a n", a=1)),
                 (xg[D + 1:D + 2, 0:NE], t["L1_ffn_bias"].rearrange("(a n) -> a n", a=1)),
                 (hid[:, :, :], tok.rearrange("(i b) r w -> (b r) i w", b=2))]
        for k in range(2):
            loads.append((wd[:, k, :].rearrange("p (e n) -> p e n", e=NE),
                          t["L0_ffn_Wd"].rearrange("e (k p) n -> k p e n", k=2)[k]))
            loads.append((wg[:, k, 0:NE], t["L0_ffn_Wg"].rearrange("(k p) n -> k p n", k=2)[k]))
            for hp in range(HP):
                loads.append((w0[64 * k:64 * k + 64, hp, D * k:D * k + D],
                              t["L0_attn_W0"].rearrange("(d h) n -> h d n", h=HEADS)[2 * hp + k]))
        with nc.Block() as block:
            @block.vector
            def _(dve):
                zeros = [wqkv[:, :], w0[:, :, :], w1[:, :], wg[:, :, :], dxt[:, :], dyt[:, :], et[:, :, :],
                         x1[:, :], xg[:, :]]
                for v in zeros:
                    dve.memset(v, 0.0).then_inc(w_zero, 1)
                dve.memset(zt[64:128, :], 1.0).then_inc(w_zero, 1)
                dve.memset(nhalf[:, :], -0.5).then_inc(w_zero, 1)
                dve.memset(ones[:, :], 1.0).then_inc(w_zero, 1)
                dve.wait_ge(w_zero, 12)
                dve.wait_ge(w_in, 16 * len(loads))
                dve.tensor_copy(wqkv[0:65, :].rearrange("p (s h d) -> p s h d", s=3, h=HEADS),
                                big[0:65, 1, 0:3 * QW].rearrange("p (s d h) -> p s h d", s=3, h=HEADS))
                dve.wait_ge(w_pe, 1)
                for k in range(2):
                    dve.tensor_copy(dxt[0:64, 128 * k:128 * k + 128], ps[0][0:64, 128 * k:128 * k + 128])
                    dve.tensor_copy(dyt[0:64, 128 * k:128 * k + 128], ps[0][0:64, 256 + 128 * k:256 + 128 * k + 128])
                    dve.tensor_copy(et[:, k, 0:D], ps[1][:, 64 * k:64 * k + 64])

            @block.sync
            def _(sp):
                sp.wait_ge(w_zero, 12)
                for dst, src in loads:
                    sp.dma_start(dst, src).then_inc(w_in, 16)

            @block.tensor
            def _(pe):
                pe.wait_ge(w_in, 16 * len(loads))
                for k in range(4):
                    pe.transpose(ps[0][0:64, 128 * k:128 * k + 128], rawd[:, k, :], ident[:, :])
                for k in range(2):
                    mm = pe.transpose(ps[1][:, 64 * k:64 * k + 64], rawe[:, 128 * k:128 * k + 128], ident[0:64, 0:64])
                mm.then_inc(w_pe, 1)

        s_sum, s_cen, s_sq, s_red, s_var, s_rstd, s_out, s_t, s_ev, s_add = sems(
            "norm", "sum", "cen", "sq", "red", "var", "rstd", "out", "t", "ev", "add")
        PARTS = 4

        def normalise(call, src, dst, residual=None, transpose=None):
            n, parts = NT // PARTS, PARTS
            p0 = call * PARTS
            t0 = (transpose or 0) * (NT // 4)
            cen = big[:, 0, 0:NT * D].rearrange("p (i d) -> p i d", d=D)
            sqr = big[:, 0, NT * D:2 * NT * D].rearrange("p (i d) -> p i d", d=D)
            with nc.Block() as block:
                @block.vector
                def _(dve):
                    for k in range(parts + 2):
                        if k < parts:
                            i = slice(n * k, n * k + n)
                            dve.tensor_reduce(stat[:, 0, i], src[:, i, :], AX.X, ALU.add).then_inc(s_sum, 1)
                            dve.wait_ge(s_sum, p0 + k + 1)
                            dve.scalar_tensor_tensor(out=cen[:, i, :], in0=stat[:, 0, i].unsqueeze(2).to_broadcast([128, n, D]),
                                                     scalar=-1.0 / D, in1=src[:, i, :], op0=ALU.mult,
                                                     op1=ALU.add).then_inc(s_cen, 1)
                        if 1 <= k <= parts:
                            i = slice(n * (k - 1), n * k)
                            dve.wait_ge(s_sq, p0 + k)
                            dve.tensor_reduce(stat[:, 1, i], sqr[:, i, :], AX.X, ALU.add).then_inc(s_red, 1)
                        if k >= 2:
                            i = slice(n * (k - 2), n * (k - 1))
                            dve.wait_ge(s_rstd, p0 + k - 1)
                            dve.tensor_tensor(dst[:, i, :], cen[:, i, :],
                                              stat[:, 3, i].unsqueeze(2).to_broadcast([128, n, D]),
                                              ALU.mult).then_inc(s_out, 1)
                            if residual is not None:
                                dve.wait_ge(s_out, p0 + k - 1)
                                dve.tensor_tensor(residual[:, i, :], residual[:, i, :], dst[:, i, :], ALU.add).then_inc(s_add, 1)
                    if transpose is not None:
                        for k in range(0, NT // 4, 2):
                            dve.wait_ge(s_t, t0 + k + 1)
                            dve.tensor_copy(zt[0:64, 512 * k:512 * k + 512], ps[k][0:64, :]).then_inc(s_ev, 1)

                @block.scalar
                def _(act):
                    for k in range(parts):
                        i = slice(n * k, n * k + n)
                        act.wait_ge(s_cen, p0 + k + 1)
                        act.activation(sqr[:, i, :], cen[:, i, :], ACT.Square).then_inc(s_sq, 1)
                    if transpose is not None:
                        for k in range(1, NT // 4, 2):
                            act.wait_ge(s_t, t0 + k + 1)
                            act.copy(zt[0:64, 512 * k:512 * k + 512], ps[k][0:64, :]).then_inc(s_ev, 1)

                @block.gpsimd
                def _(pool):
                    for k in range(parts):
                        i = slice(n * k, n * k + n)
                        pool.wait_ge(s_red, p0 + k + 1)
                        pool.tensor_scalar(stat[:, 2, i], stat[:, 1, i], 1.0 / D, EPS, ALU.mult, ALU.add).then_inc(s_var, 1)
                        pool.wait_ge(s_var, p0 + k + 1)
                        pool.tensor_tensor(stat[:, 3, i], stat[:, 2, i], nhalf[:, i], ALU.pow).then_inc(s_rstd, 1)

                if transpose is not None:
                    @block.tensor
                    def _(pe):
                        for k in range(NT // 4):
                            pe.wait_ge(s_out, p0 + k // 2 + 1)
                            for i in range(4):
                                mm = pe.transpose(ps[k][0:64, 128 * i:128 * i + 128], dst[:, 4 * k + i, :], ident[:, :])
                            mm.then_inc(s_t, 1)

        normalise(0, hid, z, transpose=0)

        def project(pe, bank, section, hp, r0):
            first = section * TOK + r0
            for seg in range(3):
                m0 = -(-(first - seg) // 3)
                m1 = (first + 511 - seg) // 3 + 1
                at = 3 * m0 + seg - first
                w = (seg * HEADS + 2 * hp) * D
                mm = pe.matmul(bank[:, at:at + 3 * (m1 - m0 - 1) + 1:3], wqkv[:, w:w + 128], zt[:, m0:m1],
                               start=True, stop=True, skip_group_check=True)
            return mm

        a_full, a_e0, a_e1 = sems("qk", "full", "free0", "free1")
        jobs = [(sec, hp, r) for r in range(0, TOK, 512) for sec in range(2) for hp in range(HP)]
        qk = big[:, :, :].rearrange("p s (h r) -> p s h r", h=HP)
        with nc.Block() as block:
            @block.tensor
            def _(pe):
                for n, (sec, hp, r) in enumerate(jobs):
                    if n >= 8:
                        pe.wait_ge((a_e0, a_e1)[n % 2], n // 2 - 3)
                    project(pe, ps[n % 8], sec, hp, r).then_inc(a_full, 1)

            @block.vector
            def _(dve):
                for n in range(0, len(jobs), 2):
                    sec, hp, r = jobs[n]
                    dve.wait_ge(a_full, n + 1)
                    dve.tensor_copy(qk[:, sec, hp, r:r + 512], ps[n % 8][:, :]).then_inc(a_e0, 1)

            @block.scalar
            def _(act):
                for n in range(1, len(jobs), 2):
                    sec, hp, r = jobs[n]
                    act.wait_ge(a_full, n + 1)
                    act.copy(qk[:, sec, hp, r:r + 512], ps[n % 8][:, :]).then_inc(a_e1, 1)

        c_full, c_max, c_sub, c_exp, c_sum, c_msk, c_dg, c_rc, c_at = sems(
            "sc", "full", "max", "sub", "exp", "sum", "msk", "dg", "rc", "at")
        NS_ = NT // 2 * 2
        shifted = lv[:, :, :].rearrange("p (b i) d -> p b (i d)", b=4)
        masked = z[:, :, :].rearrange("p (b i) d -> p b (i d)", b=4)
        G8 = [128, 8, S]
        with nc.Block() as block:
            @block.tensor
            def _(pe):
                for n in range(NS_):
                    j, par = n // 2, n % 2
                    if n >= 8:
                        pe.wait_ge(c_sub, n - 7)
                    rows = slice(64 * par, 64 * par + 64)
                    for i in range(2):
                        for b in range(2):
                            r = ((2 * j + i) * 2 + b) * S
                            for hp in range(HP):
                                col = (i * HP + hp) * S
                                mm = pe.matmul(ps[n % 8][64 * b:64 * b + 64, col:col + S], qk[rows, 1, hp, r:r + S],
                                               qk[rows, 0, hp, r:r + S], start=True, stop=True)
                    mm.then_inc(c_full, 1)

            @block.vector
            def _(dve):
                lag = 2
                for n in range(NS_ + lag):
                    if n < NS_:
                        dve.wait_ge(c_full, n + 1)
                        b = ps[n % 8][:, :].rearrange("p (g s) -> p g s", s=S)
                        mx = gates[:, 1, 8 * (n % 4):8 * (n % 4) + 8]
                        dve.tensor_reduce(mx, b, AX.X, ALU.max).then_inc(c_max, 1)
                        dve.wait_ge(c_max, n + 1)
                        if n >= 4:
                            dve.wait_ge(c_msk, n - 3)
                        dve.tensor_tensor(shifted[:, n % 4, :].rearrange("p (g s) -> p g s", s=S), b,
                                          mx.unsqueeze(2).to_broadcast(G8), ALU.subtract).then_inc(c_sub, 1)
                    if n >= lag:
                        d = n - lag
                        j, par = d // 2, d % 2
                        e = shifted[:, d % 4, :].rearrange("p (g s) -> p g s", s=S)
                        m = masked[:, d % 4, :].rearrange("p (g s) -> p g s", s=S)
                        dve.wait_ge(c_exp, d + 1)
                        dve.tensor_reduce(gates[:, 2, 8 * d:8 * d + 8], e, AX.X, ALU.add).then_inc(c_sum, 1)
                        if d >= 4:
                            dve.wait_ge(c_dg, d - 3)
                        dve.tensor_tensor(m, e, diag[:, :].unsqueeze(1).to_broadcast(G8), ALU.mult).then_inc(c_msk, 1)
                        dve.wait_ge(c_msk, d + 1)
                        dve.tensor_reduce(gates[:, 3, 8 * d:8 * d + 8], m, AX.X, ALU.add).then_inc(c_dg, 1)
                dve.wait_ge(c_sum, NS_)
                dve.reciprocal(gates[:, 4, :], gates[:, 2, :]).then_inc(c_rc, 1)
                dve.wait_ge(c_rc, 1)
                dve.wait_ge(c_dg, NS_)
                for par in range(2):
                    for i in range(2):
                        def v(k):
                            return gates[:, k, :].rearrange("p (j q i h) -> p q i j h", q=2, i=2, h=HP)[:, par, i]
                        o = gates[:, 0, :].rearrange("p (j i h q) -> p q i j h", i=2, q=2, h=HP)[:, par, i]
                        dve.tensor_tensor(o, v(3), v(4), ALU.mult).then_inc(c_at, 1)

            @block.scalar
            def _(act):
                for n in range(NS_):
                    act.wait_ge(c_sub, n + 1)
                    act.activation(shifted[:, n % 4, :], shifted[:, n % 4, :], ACT.Exp, scale=float(D) ** -0.5).then_inc(c_exp, 1)

        v_full, v_sb, v_p, v_w, v_r, v_a = sems("v", "full", "sb", "p", "w", "r", "a")
        NCK = TOK // 512
        vt = big[:, 0, 0:2 * HP * 512].rearrange("p (b h r) -> p b h r", b=2, h=HP)
        wtd = big[:, 1, 0:2 * 512].rearrange("p (b n) -> p b n", b=2)
        red = big[:, 1, 2048:2048 + 2 * D].rearrange("p (b n) -> p b n", b=2)
        with nc.Block() as block:
            @block.tensor
            def _(pe):
                for c in range(NCK + 1):
                    if c < NCK:
                        for hp in range(HP):
                            if c >= 1:
                                pe.wait_ge(v_sb, HP * (c - 1) + hp + 1)
                            project(pe, ps[hp], 2, hp, 512 * c).then_inc(v_full, 1)
                    if c >= 1:
                        for i in range(4):
                            n = 4 * (c - 1) + i
                            pe.wait_ge(v_sb, HP * c)
                            if n >= 4:
                                pe.wait_ge(v_w, n - 3)
                            for hp in range(HP):
                                mm = pe.matmul(ps[4 + n % 4][:, 128 * hp:128 * hp + 128],
                                               vt[:, (c - 1) % 2, hp, 128 * i:128 * i + 128], w0[:, hp, :], start=True, stop=True)
                            mm.then_inc(v_p, 1)

            @block.scalar
            def _(act):
                for c in range(NCK):
                    for hp in range(HP):
                        act.wait_ge(v_full, HP * c + hp + 1)
                        if c >= 2:
                            act.wait_ge(v_p, 4 * (c - 1))
                        act.copy(vt[:, c % 2, hp, :], ps[hp][:, :]).then_inc(v_sb, 1)

            @block.vector
            def _(dve):
                for n in range(NT + 3):
                    if n < NT:
                        dve.wait_ge(v_p, n + 1)
                        if n >= 2:
                            dve.wait_ge(v_r, n - 1)
                        dve.tensor_tensor(wtd[:, n % 2, :].rearrange("p (h d) -> p h d", d=D),
                                          ps[4 + n % 4][:, :].rearrange("p (h d) -> p h d", d=D),
                                          attn[:, n, :].unsqueeze(2).to_broadcast([128, HEADS, D]), ALU.mult).then_inc(v_w, 1)
                    if 1 <= n <= NT:
                        d = n - 1
                        dve.wait_ge(v_w, d + 1)
                        if d >= 2:
                            dve.wait_ge(v_a, 2 * d - 3)
                        dve.tensor_reduce(red[:, d % 2, :], wtd[:, d % 2, :].rearrange("p (h d) -> p d h", d=D), AX.X,
                                          ALU.add).then_inc(v_r, 1)
                    if n >= 3:
                        d = n - 3
                        dve.wait_ge(v_a, 2 * d + 1)
                        dve.tensor_tensor(hid[:, d, :], hid[:, d, :], b0[:, :], ALU.add).then_inc(v_a, 1)
                    if 2 <= n <= NT + 1:
                        d = n - 2
                        dve.wait_ge(v_r, d + 1)
                        dve.tensor_tensor(hid[:, d, :], hid[:, d, :], red[:, d % 2, :], ALU.add).then_inc(v_a, 1)

        def first_max(dve, sem_, count, logits, top, pick):
            v3 = lambda a: a.rearrange("p (i e) -> p i e", e=NE)
            b = lambda a: a.unsqueeze(2).to_broadcast([128, NT, NE])
            steps = [lambda: dve.tensor_reduce(top, v3(logits), AX.X, ALU.max),
                     lambda: dve.tensor_tensor(v3(pick), v3(logits), b(top), ALU.is_equal),
                     lambda: dve.tensor_tensor(v3(pick), v3(pick), rank[:, :].unsqueeze(1).to_broadcast([128, NT, NE]), ALU.mult),
                     lambda: dve.tensor_reduce(stat[:, 5, :], v3(pick), AX.X, ALU.max),
                     lambda: dve.tensor_tensor(v3(pick), v3(pick), b(stat[:, 5, :]), ALU.is_equal)]
            for step in steps:
                step().then_inc(sem_, 1)
                count += 1
                dve.wait_ge(sem_, count)
            return count

        def combine(dve, s_y, banks, bias, weights, s_b, s_w, s_r, s_a):
            def half(n, at, width=512):
                return big[:, 1, at + 1024 * (n % 2):at + 1024 * (n % 2) + width]

            def summed(n):
                return big[:, 1, 14336 + 64 * (n % 2):14336 + 64 * (n % 2) + 64]

            for n in range(NT + 3):
                if n < NT:
                    dve.wait_ge(s_y, n + 1)
                    if n >= 2:
                        dve.wait_ge(s_w, n - 1)
                    dve.tensor_tensor(half(n, 12288), banks[n % 4][:, :], bias, ALU.add).then_inc(s_b, 1)
                if 1 <= n <= NT:
                    d = n - 1
                    dve.wait_ge(s_b, d + 1)
                    if d >= 2:
                        dve.wait_ge(s_r, d - 1)
                    dve.tensor_tensor(half(d, 12800).rearrange("p (e d) -> p e d", d=D),
                                      half(d, 12288).rearrange("p (e d) -> p e d", d=D),
                                      weights[:, NE * d:NE * d + NE].unsqueeze(2).to_broadcast([128, NE, D]),
                                      ALU.mult).then_inc(s_w, 1)
                if 2 <= n <= NT + 1:
                    d = n - 2
                    dve.wait_ge(s_w, d + 1)
                    if d >= 2:
                        dve.wait_ge(s_a, d - 1)
                    dve.tensor_reduce(summed(d), half(d, 12800).rearrange("p (e d) -> p d e", d=D), AX.X, ALU.add).then_inc(s_r, 1)
                if n >= 3:
                    d = n - 3
                    dve.wait_ge(s_r, d + 1)
                    dve.tensor_tensor(hid[:, d, :], hid[:, d, :], summed(d), ALU.add).then_inc(s_a, 1)

        normalise(1, hid, z, transpose=1)
        f_full, f_h, f_g, f_lg, f_gt, f_exp, f_y, f_b, f_w, f_r, f_a = sems(
            "f", "full", "h", "g", "lg", "gt", "exp", "y", "b", "w", "r", "a")
        ht = big[:, 0, 0:2 * TOK].rearrange("p (k n) -> p k n", k=2)
        logits, top, pick, ex = gates[:, 1, :], stat[:, 4, :], gates[:, 2, :], gates[:, 3, :]
        with nc.Block() as block:
            @block.tensor
            def _(pe):
                for n in range(16):
                    if n >= 4:
                        pe.wait_ge(f_h, n - 3)
                    k, c = n % 2, n // 2
                    pe.matmul(ps[n % 4][:, :], w1[:, 128 * k:128 * k + 128], zt[:, 512 * c:512 * c + 512],
                              start=True, stop=True).then_inc(f_full, 1)
                pe.wait_ge(f_h, 16)
                for n in range(NT):
                    b, o = 4 + n // 4 % 2, 100 * (n % 4)
                    if n % 4 == 0 and n >= 8:
                        pe.wait_ge(f_lg, n // 4 - 1)
                    for k in range(2):
                        mm = pe.matmul(ps[b][:, o:o + PADN], ht[:, k, 128 * n:128 * n + 128], wg[:, k, :],
                                       start=(k == 0), stop=(k == 1))
                    if n % 4 == 3:
                        mm.then_inc(f_g, 1)
                for n in range(NT):
                    if n >= 4:
                        pe.wait_ge(f_b, n - 3)
                    for k in range(2):
                        mm = pe.matmul(ps[n % 4][:, :], ht[:, k, 128 * n:128 * n + 128], wd[:, k, :],
                                       start=(k == 0), stop=(k == 1))
                    mm.then_inc(f_y, 1)

            @block.scalar
            def _(act):
                for n in range(16):
                    act.wait_ge(f_full, n + 1)
                    act.activation(ht[:, n % 2, 512 * (n // 2):512 * (n // 2) + 512], ps[n % 4][:, :], ACT.Gelu).then_inc(f_h, 1)
                act.wait_ge(f_gt, 6)
                act.activation(ex, ex, ACT.Exp).then_inc(f_exp, 1)

            @block.vector
            def _(dve):
                v3 = lambda a: a.rearrange("p (i e) -> p i e", e=NE)
                for n in range(NT // 4):
                    dve.wait_ge(f_g, n + 1)
                    dve.tensor_tensor(v3(logits)[:, 4 * n:4 * n + 4, :],
                                      ps[4 + n % 2][:, 0:400].rearrange("p (i e) -> p i e", i=4)[:, :, 0:NE],
                                      bg[:, :].unsqueeze(1).to_broadcast([128, 4, NE]), ALU.add).then_inc(f_lg, 1)
                dve.wait_ge(f_lg, NT // 4)
                count = first_max(dve, f_gt, 0, logits, top, pick)
                b = lambda a: a.unsqueeze(2).to_broadcast([128, NT, NE])
                dve.tensor_tensor(v3(ex), v3(logits), b(top), ALU.subtract).then_inc(f_gt, 1)
                dve.wait_ge(f_exp, 1)
                dve.tensor_reduce(stat[:, 0, :], v3(ex), AX.X, ALU.add).then_inc(f_gt, 1)
                dve.wait_ge(f_gt, count + 2)
                dve.reciprocal(stat[:, 1, :], stat[:, 0, :]).then_inc(f_gt, 1)
                dve.wait_ge(f_gt, count + 3)
                dve.tensor_tensor(v3(pick), v3(pick), b(stat[:, 1, :]), ALU.mult).then_inc(f_gt, 1)
                dve.wait_ge(f_gt, count + 4)
                combine(dve, f_y, ps[0:4], bd[:, :], pick, f_b, f_w, f_r, f_a)

        normalise(2, hid, z, transpose=2)
        normalise(3, z, lv)
        r_full, r_x, r_rf, r_rs, r_s, r_d, r_b, r_sc = sems("r", "full", "x", "rf", "rs", "s", "d", "b", "sc")
        rt = big[:, 0, 0:2 * TOK].rearrange("p (k n) -> p k n", k=2)
        rb = big[:, 0, 2 * TOK:3 * TOK]
        ss = big[:, 0, 3 * TOK:4 * TOK]
        av = big[:, 1, 0:TOK]
        rec = big[:, 1, TOK:2 * TOK]
        xt = big[:, 1, 2 * TOK:4 * TOK].rearrange("p (k n) -> p k n", k=2)
        cbuf = stat[:, 0:2, :].rearrange("p a n -> p (a n)")
        with nc.Block() as block:
            @block.tensor
            def _(pe):
                for n in range(16):
                    if n >= 4:
                        pe.wait_ge(r_x, n - 3)
                    k, c = n % 2, n // 2
                    pe.matmul(ps[n % 4][:, :], dxt[:, 128 * k:128 * k + 128], zt[:, 512 * c:512 * c + 512],
                              start=True, stop=True).then_inc(r_full, 1)
                for c in range(8):
                    pe.wait_ge(r_x, 2 * c + 2)
                    if c >= 4:
                        pe.wait_ge(r_rs, c - 3)
                    for k in range(2):
                        mm = pe.matmul(ps[4 + c % 4][:, :], ones[:, :], rt[:, k, 512 * c:512 * c + 512],
                                       start=(k == 0), stop=(k == 1))
                    mm.then_inc(r_rf, 1)

            @block.scalar
            def _(act):
                for n in range(16):
                    act.wait_ge(r_full, n + 1)
                    act.activation(rt[:, n % 2, 512 * (n // 2):512 * (n // 2) + 512], ps[n % 4][:, :], ACT.Relu).then_inc(r_x, 1)
                for c in range(8):
                    act.wait_ge(r_rf, c + 1)
                    act.copy(rb[:, 512 * c:512 * c + 512], ps[4 + c % 4][:, :]).then_inc(r_rs, 1)

            @block.vector
            def _(dve):
                sv = ss.rearrange("p (b t) -> p t b", t=S)
                rv = rb.rearrange("p (b t) -> p t b", t=S)
                dve.wait_ge(r_rs, 8)
                dve.tensor_copy(sv[:, 0, :], rv[:, 0, :]).then_inc(r_s, 1)
                for i in range(1, S):
                    dve.wait_ge(r_s, 2 * i - 1)
                    dve.tensor_scalar(cbuf, sv[:, i - 1, :], DECAY / L1_EPS, DECAY, ALU.mult, ALU.min).then_inc(r_s, 1)
                    dve.wait_ge(r_s, 2 * i)
                    dve.tensor_tensor(sv[:, i, :], cbuf, rv[:, i, :], ALU.add).then_inc(r_s, 1)
                dve.wait_ge(r_s, 2 * S - 1)
                dve.tensor_scalar(ss, ss, L1_EPS, None, ALU.max).then_inc(r_d, 1)
                dve.wait_ge(r_d, 1)
                dve.reciprocal(rec, ss).then_inc(r_d, 1)
                dve.wait_ge(r_d, 2)
                dve.tensor_scalar(av, rec, DECAY, None, ALU.mult).then_inc(r_d, 1)
                dve.wait_ge(r_d, 3)
                dve.memset(av.rearrange("p (b t) -> p t b", t=S)[:, 0, :], 0.0).then_inc(r_d, 1)
                for k in range(2):
                    dve.tensor_tensor(rt[:, k, :], rt[:, k, :], rec, ALU.mult).then_inc(r_b, 1)
                dve.wait_ge(r_d, 4)
                dve.wait_ge(r_b, 2)
                for k in range(2):
                    dve.tensor_tensor_scan(xt[:, k, :], av, rt[:, k, :], 0.0, ALU.mult, ALU.add).then_inc(r_sc, 1)

        g_full, g_m, g_a, g_ev = sems("g", "full", "m", "a", "ev")
        gm = big[:, 0, 0:NT * S].rearrange("p (i t) -> p i t", t=S)
        with nc.Block() as block:
            @block.tensor
            def _(pe):
                for c in range(NT // 8):
                    for i in range(8):
                        for b in range(2):
                            n = ((8 * c + i) * 2 + b) * S
                            for k in range(2):
                                mm = pe.matmul(ps[c][64 * b:64 * b + 64, S * i:S * i + S], xt[:, k, n:n + S], xt[:, k, n:n + S],
                                               start=(k == 0), stop=(k == 1))
                    mm.then_inc(g_full, 1)
                for b in range(2):
                    for c in range(NT // 8):
                        if b:
                            pe.wait_ge(g_ev, c + 1)
                        pe.wait_ge(g_m, c + 1)
                        rows = slice(64 * b, 64 * b + 64)
                        for i in range(8):
                            n = 8 * c + i
                            mm = pe.matmul(ps[4 + c][rows, D * i:D * i + D], gm[rows, n, :], lv[rows, n, :], start=True, stop=True)
                        mm.then_inc(g_a, 1)

            @block.vector
            def _(dve):
                for c in range(NT // 8):
                    dve.wait_ge(g_full, c + 1)
                    dve.tensor_tensor(gm[:, 8 * c:8 * c + 8, :], ps[c][:, :].rearrange("p (i t) -> p i t", t=S),
                                      decay[:, :].unsqueeze(1).to_broadcast([128, 8, S]), ALU.mult).then_inc(g_m, 1)
                for b in range(2):
                    for c in range(NT // 8):
                        dve.wait_ge(g_a, (NT // 8) * b + c + 1)
                        rows = slice(64 * b, 64 * b + 64)
                        dve.tensor_copy(z[rows, 8 * c:8 * c + 8, :], ps[4 + c][rows, :].rearrange("p (i d) -> p i d", d=D)).then_inc(g_ev, 1)

        normalise(4, z, lv, transpose=3)
        y_full, y_y, y_v, y_ev = sems("y", "full", "y", "v", "ev")
        yt = big[:, 0, 0:2 * TOK].rearrange("p (k n) -> p k n", k=2)
        with nc.Block() as block:
            @block.tensor
            def _(pe):
                for n in range(16):
                    if n >= 4:
                        pe.wait_ge(y_y, n - 3)
                    k, c = n % 2, n // 2
                    pe.matmul(ps[n % 4][:, :], dyt[:, 128 * k:128 * k + 128], zt[:, 512 * c:512 * c + 512],
                              start=True, stop=True).then_inc(y_full, 1)
                for n in range(NT):
                    pe.wait_ge(y_y, 2 * (n // 4) + 2)
                    if n % 4 == 0 and n >= 16:
                        pe.wait_ge(y_ev, n // 4 - 3)
                    o = ps[4 + n // 4 % 4][:, 100 * (n % 4):100 * (n % 4) + PADN]
                    for k in range(2):
                        mm = pe.matmul(o, yt[:, k, 128 * n:128 * n + 128], et[:, k, :], start=(k == 0), stop=(k == 1))
                    if n % 4 == 3:
                        mm.then_inc(y_v, 1)

            @block.vector
            def _(dve):
                for n in range(16):
                    dve.wait_ge(y_full, n + 1)
                    k, c = n % 2, slice(512 * (n // 2), 512 * (n // 2) + 512)
                    dve.scalar_tensor_tensor(out=yt[:, k, c], in0=ps[n % 4][:, :], scalar=0.0, in1=xt[:, k, c],
                                             op0=ALU.max, op1=ALU.mult).then_inc(y_y, 1)

            @block.scalar
            def _(act):
                for n in range(NT // 4):
                    act.wait_ge(y_v, n + 1)
                    act.copy(z[:, 4 * n:4 * n + 4, :],
                             ps[4 + n % 4][:, 0:400].rearrange("p (i d) -> p i d", i=4)[:, :, 0:D]).then_inc(y_ev, 1)

        normalise(5, z, lv, residual=hid)
        normalise(6, hid, z, transpose=4)
        e_g, e_lg, e_gt, e_exp, e_full, e_h, e_y, e_b, e_w, e_r, e_a, e_out = sems(
            "e", "g", "lg", "gt", "exp", "full", "h", "y", "b", "w", "r", "a", "out")
        logits2, pick2, cmb = gates[:, 4, :], gates[:, 5, :], gates[:, 6, :]
        eh = big[:, 0, 0:2 * NE * 512].rearrange("p (b e n) -> p b e n", b=2, e=NE)
        with nc.Block() as block:
            @block.tensor
            def _(pe):
                for n in range(NT):
                    b, o = 4 + n // 4 % 4, 100 * (n % 4)
                    if n % 4 == 0 and n >= 16:
                        pe.wait_ge(e_lg, n // 4 - 3)
                    mm = pe.matmul(ps[b][:, o:o + PADN], zt[:, 128 * n:128 * n + 128], xg[:, :], start=True, stop=True)
                    if n % 4 == 3:
                        mm.then_inc(e_g, 1)
                pe.wait_ge(e_lg, NT // 4)
                for c in range(NCK + 1):
                    if c < NCK:
                        for e in range(NE):
                            n = NE * c + e
                            if n >= 4:
                                pe.wait_ge(e_h, n - 3)
                            pe.matmul(ps[n % 4][:, :], x1[:, ED * e:ED * e + ED], zt[:, 512 * c:512 * c + 512],
                                      start=True, stop=True).then_inc(e_full, 1)
                    if c >= 1:
                        for i in range(4):
                            n = 4 * (c - 1) + i
                            pe.wait_ge(e_h, NE * c)
                            if n >= 4:
                                pe.wait_ge(e_b, n - 3)
                            for e in range(NE):
                                w = PADN if e < NE - 1 else D
                                mm = pe.matmul(ps[4 + n % 4][:, D * e:D * e + w], eh[:, (c - 1) % 2, e, 128 * i:128 * i + 128],
                                               x2[:, :, :].rearrange("p e d -> p (e d)")[:, D * e:D * e + w],
                                               start=True, stop=True, skip_group_check=True)
                            mm.then_inc(e_y, 1)

            @block.scalar
            def _(act):
                act.wait_ge(e_gt, 14)
                act.activation(stat[:, 3, :], stat[:, 2, :], ACT.Exp).then_inc(e_exp, 1)
                for n in range(NE * NCK):
                    c, e = n // NE, n % NE
                    act.wait_ge(e_full, n + 1)
                    if c >= 2:
                        act.wait_ge(e_y, 4 * (c - 1))
                    act.activation(eh[:, c % 2, e, :], ps[n % 4][:, :], ACT.Relu).then_inc(e_h, 1)

            @block.vector
            def _(dve):
                v3 = lambda a: a.rearrange("p (i e) -> p i e", e=NE)
                b = lambda a: a.unsqueeze(2).to_broadcast([128, NT, NE])
                for n in range(NT // 4):
                    dve.wait_ge(e_g, n + 1)
                    dve.tensor_copy(v3(logits)[:, 4 * n:4 * n + 4, :],
                                    ps[4 + n % 4][:, 0:400].rearrange("p (i e) -> p i e", i=4)[:, :, 0:NE]).then_inc(e_lg, 1)
                dve.wait_ge(e_lg, NT // 4)
                count = first_max(dve, e_gt, 0, logits, stat[:, 0, :], pick)
                dve.tensor_scalar(pick2, pick, -1e30, None, ALU.mult).then_inc(e_gt, 1)
                dve.wait_ge(e_gt, count + 1)
                dve.tensor_tensor(logits2, logits, pick2, ALU.add).then_inc(e_gt, 1)
                count += 2
                dve.wait_ge(e_gt, count)
                count = first_max(dve, e_gt, count, logits2, stat[:, 1, :], pick2)
                dve.tensor_tensor(stat[:, 2, :], stat[:, 1, :], stat[:, 0, :], ALU.subtract).then_inc(e_gt, 1)
                dve.wait_ge(e_gt, count + 1)
                dve.tensor_copy(stat[:, 4, :], stat[:, 2, :]).then_inc(e_gt, 1)
                count += 2
                dve.wait_ge(e_exp, 1)
                steps = [lambda: dve.tensor_scalar(stat[:, 4, :], stat[:, 3, :], 1.0, None, ALU.add),
                         lambda: dve.reciprocal(stat[:, 5, :], stat[:, 4, :]),
                         lambda: dve.tensor_tensor(stat[:, 4, :], stat[:, 5, :], stat[:, 3, :], ALU.mult),
                         lambda: dve.tensor_tensor(v3(pick), v3(pick), b(stat[:, 5, :]), ALU.mult),
                         lambda: dve.tensor_tensor(v3(pick2), v3(pick2), b(stat[:, 4, :]), ALU.mult),
                         lambda: dve.tensor_tensor(cmb, pick, pick2, ALU.add)]
                dve.wait_ge(e_gt, count)
                for step in steps:
                    step().then_inc(e_gt, 1)
                    count += 1
                    dve.wait_ge(e_gt, count)
                combine(dve, e_y, ps[4:8], x2b[:, :], cmb, e_b, e_w, e_r, e_a)

            @block.sync
            def _(sp):
                for c in range(NT // 8):
                    sp.wait_ge(e_a, 8 * c + 8)
                    sp.dma_start(out.rearrange("(i b) r w -> (b r) i w", b=2)[:, 8 * c:8 * c + 8, :],
                                 hid[:, 8 * c:8 * c + 8, :]).then_inc(e_out, 16)
                sp.wait_ge(e_out, 16 * (NT // 8))


def build(nc, t, out):
    tok = nc.dram_tensor("tok", (IMGS, S, S), F32, kind="Internal").ap()
    with ExitStack() as named:
        tokenizer(nc, t, tok, named)
        blocks(nc, t, tok, out, named)


_INS = ['x', 'L0_tok_fc0_w', 'L0_tok_fc0_b', 'L0_tok_ln0_g', 'L0_tok_ln0_b', 'L0_tok_w1r', 'L0_tok_w1i', 'L0_tok_w2r',
        'L0_tok_w2i', 'L0_tok_conv_w', 'L0_tok_conv_b', 'L0_tok_ln_g', 'L0_tok_ln_b', 'L0_tok_fc1_w', 'L0_tok_fc1_b',
        'L0_tok_fc2_w', 'L0_tok_fc2_b', 'L0_tok_fc3_w', 'L0_tok_fc3_b', 'L0_attn_Wqkv', 'L0_attn_bqkv', 'L0_attn_W0',
        'L0_attn_b0', 'L0_ffn_W1', 'L0_ffn_b1', 'L0_ffn_Wg', 'L0_ffn_bg', 'L0_ffn_Wd', 'L0_ffn_bd', 'L1_attn_E',
        'L1_attn_Dx', 'L1_attn_Dy', 'L1_ffn_Wg', 'L1_ffn_bg', 'L1_ffn_bias', 'L1_ffn_W1', 'L1_ffn_b1', 'L1_ffn_W2',
        'L1_ffn_b2']


def kernel(**inputs):
    import numpy as _np
    import concourse.bacc as _bacc
    from concourse import mybir as _mybir
    from concourse.bass_utils import run_bass_kernel_spmd as _run

    nc = _bacc.Bacc("TRN2", target_bir_lowering=False, num_devices=1)
    arrays, t = {}, {}
    given = {name: _np.ascontiguousarray(inputs[name]) for name in _INS}
    given.update(tables())
    for name, a in given.items():
        arrays[f"in_{name}"] = a
        t[name] = nc.dram_tensor(f"in_{name}", a.shape, _mybir.dt.from_np(a.dtype), kind="ExternalInput").ap()
    out = nc.dram_tensor("out", (IMGS, S, S), F32, kind="ExternalOutput").ap()
    build(nc, t, out)
    r = _run(nc, [arrays], core_ids=[0])
    return r.results[0]["out"]
```
